# Optimizing a Trainium2 kernel written in Bass

```python
import numpy as np
import jax
import jax.numpy as jnp

def _softmax(x, axis=-1):
    return jax.nn.softmax(x, axis=axis)

def _gelu(x):
    return jax.nn.gelu(x, approximate=True)

def _silu(x):
    return jax.nn.silu(x)

def _sigmoid(x):
    return jax.nn.sigmoid(x)

def _layernorm(x, axis=-1, eps=1e-05):
    m = jnp.mean(x, axis=axis, keepdims=True)
    v = jnp.var(x, axis=axis, keepdims=True)
    return (x - m) / jnp.sqrt(v + eps)

def _scatter_add(tgt, idx, src, axis=0):
    return tgt.at[idx].add(src)

def _segment_sum(src, seg, n):
    return jax.ops.segment_sum(src, seg, n)
kernel_name = 'mk_decoder_postln_d1_seqx_r8_ea651d'

def setup_inputs(seed: int=0):
    np.random.seed(seed)
    _w = jnp.asarray

    def _rec_inputs():
        import jax
        import jax.numpy as jnp
        _rk = jax.random.key(seed)
        x = 7.22e-05 + 1 * jax.random.normal(jax.random.fold_in(_rk, 1), (16, 128, 256), jnp.float32)
        _lenS = 128 - jax.random.randint(jax.random.fold_in(_rk, 7), (16,), 0, max(1, 128 // 4) + 1, jnp.int32)
        _lenS2 = 128 - jax.random.randint(jax.random.fold_in(_rk, 8), (16,), 0, max(1, 128 // 4) + 1, jnp.int32)
        _ctx_2048P = jax.random.normal(jax.random.fold_in(_rk, 11), (16, 16, 256), jnp.float32)
        _ctx_2048c = jax.random.dirichlet(jax.random.fold_in(_rk, 511), 0.3 * jnp.ones((16,), jnp.float32), (16, 128))
        _ctx_2048t = jnp.einsum('bsk,bkd->bsd', _ctx_2048c, _ctx_2048P)
        _ctx_2048t = _ctx_2048t * jax.lax.rsqrt(jnp.mean(jnp.square(_ctx_2048t)) + 1e-12) * 0.953939
        ctx_2048 = 4.13588e-05 + 0.999923 * (_ctx_2048t + 0.3 * jax.random.normal(jax.random.fold_in(_rk, 611), (16, 128, 256), jnp.float32))
        return (x, ctx_2048)
    x, ctx_2048 = _rec_inputs()

    def _L0_attn_setup():
        import jax, jax.numpy as jnp
        import numpy as np
        NUM_HEADS = 16

        def _l2_normalize_complex(z):
            n = jnp.sqrt(jnp.sum(jnp.abs(z) ** 2, axis=-1, keepdims=True))
            return z / n
        key = jax.random.key(seed)
        k1, k2, k3, k4 = jax.random.split(key, 4)
        B, S, D = (4, 512, 256)
        scale = 1.0 / np.sqrt(D)
        return {'x': jax.random.normal(k1, (B, S, D), dtype=jnp.float32), 'W_q': jax.random.normal(k2, (D, D), dtype=jnp.float32) * scale, 'W_kv': jax.random.normal(k3, (D, D), dtype=jnp.float32) * scale, 'W_o': jax.random.normal(k4, (D, D), dtype=jnp.float32) * scale}
    _L0_attn_all = _L0_attn_setup()
    _L0_attn_in = {k: v for k, v in _L0_attn_all.items() if k in ('W_q', 'W_kv', 'W_o')}
    del _L0_attn_all

    def _L0_xattn_setup():
        import math
        import jax, jax.numpy as jnp
        import numpy as np
        HEADS = 16
        MASKED_BIAS = -10000.0

        def _mha(q, k, v):
            B, Sq, D = q.shape
            Sk = k.shape[-2]
            hd = D // HEADS
            qh = q.reshape(B, Sq, HEADS, hd).transpose(0, 2, 1, 3)
            kh = k.reshape(B, Sk, HEADS, hd).transpose(0, 2, 1, 3)
            vh = v.reshape(B, Sk, HEADS, hd).transpose(0, 2, 1, 3)
            scores = jnp.einsum('bhqd,bhkd->bhqk', qh, kh) / math.sqrt(hd)
            qi = jnp.arange(Sq)[:, None] + (Sk - Sq)
            ki = jnp.arange(Sk)[None, :]
            causal = ki <= qi
            scores = jnp.where(causal[None, None], scores, jnp.asarray(MASKED_BIAS, scores.dtype))
            attn = jax.nn.softmax(scores, axis=-1)
            out = jnp.einsum('bhqk,bhkd->bhqd', attn, vh)
            return out.transpose(0, 2, 1, 3).reshape(B, Sq, D)
        key = jax.random.key(seed)
        kq, kk, kv = jax.random.split(key, 3)
        B, S, D = (4, 128, 256)
        q = jax.random.normal(kq, (B, S, D), dtype=jnp.float32)
        k = jax.random.normal(kk, (B, S, D), dtype=jnp.float32)
        v = jax.random.normal(kv, (B, S, D), dtype=jnp.float32)
        return {'q': q, 'k': k, 'v': v}
    _L0_xattn_all = _L0_xattn_setup()
    _L0_xattn_in = {k: v for k, v in _L0_xattn_all.items() if k in ()}
    del _L0_xattn_all

    def _L0_ffn_setup():
        import jax, jax.numpy as jnp
        import numpy as np

        def ternary_quantize(t, threshold, scale):
            return jnp.where(t > threshold, scale, jnp.where(t < -threshold, -scale, 0.0)).astype(t.dtype)
        key = jax.random.key(seed)
        k1, k2, k3 = jax.random.split(key, 3)
        B, S, D = (4, 512, 256)
        x = jax.random.normal(k1, (B, S, D), dtype=jnp.float32)
        weight = jax.random.normal(k2, (D, D), dtype=jnp.float32) * 0.02
        rram_variation = jax.random.normal(k3, (D, D), dtype=jnp.float32) * 0.05
        return {'x': x, 'weight': weight, 'rram_variation': rram_variation}
    _L0_ffn_all = _L0_ffn_setup()
    _L0_ffn_in = {k: v for k, v in _L0_ffn_all.items() if k in ('weight', 'rram_variation')}
    del _L0_ffn_all
    return {'x': x, 'ctx_2048': ctx_2048, 'L0_attn_W_q': _L0_attn_in['W_q'], 'L0_attn_W_kv': _L0_attn_in['W_kv'], 'L0_attn_W_o': _L0_attn_in['W_o'], 'L0_ffn_weight': _L0_ffn_in['weight'], 'L0_ffn_rram_variation': _L0_ffn_in['rram_variation']}

def reference(x, ctx_2048, L0_attn_W_q, L0_attn_W_kv, L0_attn_W_o, L0_ffn_weight, L0_ffn_rram_variation):
    import jax
    import jax.numpy as jnp

    def _L0_attn_ref(x, W_q, W_kv, W_o):
        import jax, jax.numpy as jnp
        import numpy as np
        NUM_HEADS = 16

        def _l2_normalize_complex(z):
            n = jnp.sqrt(jnp.sum(jnp.abs(z) ** 2, axis=-1, keepdims=True))
            return z / n
        B, S, D = x.shape
        H = NUM_HEADS
        hd = D // H
        q = (x @ W_q.T).reshape(B, S, H, hd)
        kv = (x @ W_kv.T).reshape(B, S, H, hd)
        qf = jnp.fft.fft(q, axis=-1)
        kvf = jnp.fft.fft(kv, axis=-1)
        qf = _l2_normalize_complex(qf)
        kvf = _l2_normalize_complex(kvf)
        kvf = jnp.cumsum(kvf, axis=1)
        qv = qf * kvf
        values_hat = jnp.fft.ifft(qv, axis=-1).real.astype(x.dtype)
        values_hat = values_hat.reshape(B, S, D)
        return values_hat @ W_o.T

    def _L0_xattn_ref(q, k, v):
        import math
        import jax, jax.numpy as jnp
        import numpy as np
        HEADS = 16
        MASKED_BIAS = -10000.0

        def _mha(q, k, v):
            B, Sq, D = q.shape
            Sk = k.shape[-2]
            hd = D // HEADS
            qh = q.reshape(B, Sq, HEADS, hd).transpose(0, 2, 1, 3)
            kh = k.reshape(B, Sk, HEADS, hd).transpose(0, 2, 1, 3)
            vh = v.reshape(B, Sk, HEADS, hd).transpose(0, 2, 1, 3)
            scores = jnp.einsum('bhqd,bhkd->bhqk', qh, kh) / math.sqrt(hd)
            qi = jnp.arange(Sq)[:, None] + (Sk - Sq)
            ki = jnp.arange(Sk)[None, :]
            causal = ki <= qi
            scores = jnp.where(causal[None, None], scores, jnp.asarray(MASKED_BIAS, scores.dtype))
            attn = jax.nn.softmax(scores, axis=-1)
            out = jnp.einsum('bhqk,bhkd->bhqd', attn, vh)
            return out.transpose(0, 2, 1, 3).reshape(B, Sq, D)
        return _mha(q, k, v)

    def _L0_ffn_ref(x, weight, rram_variation):
        import jax, jax.numpy as jnp
        import numpy as np

        def ternary_quantize(t, threshold, scale):
            return jnp.where(t > threshold, scale, jnp.where(t < -threshold, -scale, 0.0)).astype(t.dtype)
        TH_X, SC_X = (0.33, 0.5)
        TH_W, SC_W = (0.2, 0.6)
        x_q = ternary_quantize(x, TH_X, SC_X)
        w_q = ternary_quantize(weight, TH_W, SC_W)
        w_rram = w_q + rram_variation
        return jnp.einsum('bsd,od->bso', x_q, w_rram)
    x = _layernorm(x + _L0_attn_ref(x, L0_attn_W_q, L0_attn_W_kv, L0_attn_W_o), axis=-1)
    x = _layernorm(x + _L0_xattn_ref(x, ctx_2048, ctx_2048), axis=-1)
    x = _layernorm(x + _L0_ffn_ref(x, L0_ffn_weight, L0_ffn_rram_variation), axis=-1)
    return x

_drawn_inputs = setup_inputs


def setup_inputs(seed=0):
    import zlib

    import numpy as np

    out = dict(_drawn_inputs(seed))
    spreads = {}
    factors = {}
    for name, (base, spread) in spreads.items():
        noise = np.random.default_rng([zlib.crc32(name.encode()), seed]).standard_normal(out[name].shape)
        drawn = base * np.exp(spread * noise) if base else spread * noise
        out[name] = jnp.asarray(drawn.astype(out[name].dtype))
    for name, factor in factors.items():
        out[name] = (out[name] * factor).astype(out[name].dtype)
    return out
```

```python
import concourse.bass as bass
from concourse import mybir
from contextlib import ExitStack

BATCH, TOK, DIM, HEADS = 16, 128, 256, 16
HD = DIM // HEADS
BINS = HD // 2
HALF = DIM // 2
SLOT = 32
GROUPS = HEADS * SLOT // 128
GH = HEADS // GROUPS
CHUNKS = GROUPS
CW = GH * TOK
VW = HD + 1
LN_EPS = 1e-5
TH_X, TH_W, SC_W = 0.33, 0.2, 0.6
MASK = -1e30


class Step:

    def __init__(self, eng, b=None, pair=None, odd=0):
        self.eng, self.b, self.pair, self.odd, self.held = eng, b, pair, odd, {}
        self.par = (b if b is not None else 1 + odd) % 2

    def done(self, off):
        if self.b is not None:
            return max(0, self.b + off)
        if off not in self.held:
            self.held[off] = self.eng.snap(2 * self.pair + (1 + self.odd + off))
        return self.held[off]

    def filled(self, off, dmas):
        if self.b is not None:
            return 16 * dmas * ((self.b + off) // 2 + 1)
        key = (off, dmas)
        if key not in self.held:
            self.held[key] = self.eng.snap(16 * dmas * self.pair + 16 * dmas * ((1 + self.odd + off) // 2 + 1))
        return self.held[key]

    def batch(self, off):
        return self.b + off if self.b is not None else 2 * self.pair + (1 + self.odd + off)


def steps(eng, step):
    step(Step(eng, -1), True, False, False)
    step(Step(eng, 0), True, True, False)
    with eng.Fori(0, (BATCH - 2) // 2) as pair:
        for odd in range(2):
            step(Step(eng, None, pair, odd), True, True, True)
    step(Step(eng, BATCH - 1), False, True, True)
    step(Step(eng, BATCH), False, False, True)


def decoder_layer(nc, x, xT, ctxK, ctxV, w_q, w_kv, w_oT, ffn_wT, ffn_vT, dft, idftT, upto, maskneg, ident, out):
    f32, bf16 = mybir.dt.float32, mybir.dt.bfloat16
    ALU, ACT, AX = mybir.AluOpType, mybir.ActivationFunctionType, mybir.AxisListType

    with ExitStack() as stack:
        def sb(name, shape, dt=f32):
            return stack.enter_context(nc.sbuf_tensor(name, shape, dt))

        def bank(name, shape, dt=f32):
            return stack.enter_context(nc.psum_tensor(name, shape, dt))

        def sem(name):
            return stack.enter_context(nc.semaphore(name))

        wq_s, wkv_s, woT_s = (sb(n, [128, 2, DIM]) for n in ("wq_s", "wkv_s", "woT_s"))
        dft_s, idftT_s = sb("dft_s", [128, 2, DIM]), sb("idftT_s", [128, 2, DIM])
        upto_s, mask_s, ident_s = sb("upto_s", [128, TOK]), sb("mask_s", [128, TOK]), sb("ident_s", [128, 128])
        mask_b, ident_b = sb("mask_b", [128, TOK], bf16), sb("ident_b", [128, 128], bf16)
        w_in = sb("w_in", [128, 2, 2 * DIM])
        w_out = sb("w_out", [128, 2, DIM])
        fw_s, fv_s = sb("fw_s", [128, 2, DIM]), sb("fv_s", [128, 2, DIM])
        fa, fb = sb("fa", [128, 2, DIM]), sb("fb", [128, 2, DIM])
        w_ffn = [sb(f"w_ffn{i}", [128, 2, DIM], bf16) for i in range(3)]

        x_s = [sb(f"x_s{i}", [128, DIM]) for i in range(2)]
        xT_s = [sb(f"xT_s{i}", [128, 2, TOK]) for i in range(2)]
        keys = [sb(f"keys{i}", [128, HEADS, TOK]) for i in range(2)]
        keys_b = [sb(f"keys_b{i}", [128, HEADS, TOK], bf16) for i in range(2)]
        vals = [sb(f"vals{i}", [128, HEADS, VW]) for i in range(2)]

        sq = sb("sq", [128, 2 * DIM])
        ssq, lnA, rsA, nA, rnA = (sb(n, [128, 2 * HEADS]) for n in ("ssq", "lnA", "rsA", "nA", "rnA"))
        unit = sb("unit", [128, 2, 2 * BINS, HEADS])
        y = sb("y", [128, 2, BINS, HEADS])
        cross = sb("cross", [128, 2, BINS - 1, HEADS])
        yT_s = sb("yT_s", [128, 2, TOK])
        r1, r2, r3 = sb("r1", [128, DIM]), sb("r2", [128, DIM]), sb("r3", [128, DIM])
        x1 = [sb(f"x1_{i}", [128, HEADS, SLOT]) for i in range(2)]
        x1_b = sb("x1_b", [128, HEADS, SLOT], bf16)
        x1T_b = sb("x1T_b", [128, GROUPS, TOK], bf16)
        x1T = sb("x1T", [128, GROUPS, TOK])
        probs = sb("probs", [128, HEADS, TOK])
        rden = sb("rden", [128, HEADS])
        att = sb("att", [128, DIM])
        x2 = sb("x2", [128, DIM])
        above, xq = sb("above", [128, DIM], bf16), sb("xq", [128, DIM], bf16)
        xqT_s = sb("xqT_s", [128, 2, TOK], bf16)
        res = [sb(f"res{i}", [128, DIM]) for i in range(2)]
        st = [sb(f"st{i}", [128, 6]) for i in range(3)]
        mv = [sb(f"mv{i}", [128, 2]) for i in range(3)]
        lnv, rs0, nt, rstd = ([sb(f"{n}{i}", [128, 1]) for i in range(3)] for n in ("lnv", "rs0", "nt", "rstd"))
        shift3 = sb("shift3", [128, 1])
        eps = sb("eps", [128, 1])

        p_proj = bank("p_proj", [128, 2 * DIM])
        p_sum = bank("p_sum", [128, 2, DIM])
        p_tr = bank("p_tr", [128, GROUPS, TOK])
        p_pv = bank("p_pv", [128, 512])
        p_st = [bank(f"p_st{i}", [128, CW]) for i in range(2)]
        p_ap = [bank(f"p_ap{i}", [128, CW]) for i in range(2)]
        p_trb = p_tr[:].rearrange("p a b -> p (a b)").bitcast(bf16)[:, 0:CW].rearrange("p (a b) -> p a b", a=GROUPS)
        pv = p_pv[:, 0:HEADS * VW].rearrange("p (h w) -> p h w", h=HEADS)

        in_fold, in_out, in_const, in_ffn = (sem(n) for n in ("in_fold", "in_out", "in_const", "in_ffn"))
        x_in = [sem(f"x_in{i}") for i in range(2)]
        kv_in = [sem(f"kv_in{i}") for i in range(2)]
        kb_in = [sem(f"kb_in{i}") for i in range(2)]
        stored = [sem(f"stored{i}") for i in range(2)]
        zeroed, slots_ready, folded, w_in_ready, w_out_ready, const_b, ffn_seq = (
            sem(n) for n in ("zeroed", "slots_ready", "folded", "w_in_ready", "w_out_ready", "const_b", "ffn_seq"))
        (proj, cum, yT, outA, x1T_b_done, x1T_done, xqT, ffn) = (
            sem(n) for n in ("proj", "cum", "yT", "outA", "x1T_b_done", "x1T_done", "xqT", "ffn"))
        approx = [sem(f"approx{c}") for c in range(CHUNKS)]
        scored = [sem(f"scored{c}") for c in range(CHUNKS)]
        pv_done = [sem(f"pv_done{c}") for c in range(CHUNKS)]
        (squared, lnA_done, rsA_done, yT_copied, x1_b_done, x1T_b_copied, x1T_copied, xqT_copied, out_ready) = (
            sem(n) for n in ("squared", "lnA_done", "rsA_done", "yT_copied", "x1_b_done", "x1T_b_copied",
                             "x1T_copied", "xqT_copied", "out_ready"))
        ln_done = [sem(f"ln_done{i}") for i in range(3)]
        rs_done = [sem(f"rs_done{i}") for i in range(3)]
        exps = [sem(f"exps{c}") for c in range(CHUNKS)]
        masked = [sem(f"masked{c}") for c in range(CHUNKS)]
        (ssq_done, nA1, nA2, rnA_done, normed, straight, crossed, y_cos, y_done, shift_done, rden_done, att_done,
         x1_done, x2_done, above_done, xq_done) = (
            sem(n) for n in ("ssq_done", "nA1", "nA2", "rnA_done", "normed", "straight", "crossed", "y_cos",
                             "y_done", "shift_done", "rden_done", "att_done", "x1_done", "x2_done",
                             "above_done", "xq_done"))
        added, stats, var, nt1, nt2, rstd_done = ([sem(f"{n}{i}") for i in range(3)]
                                                  for n in ("added", "stats", "var", "nt1_", "nt2_", "rstd_done"))
        maxed = [sem(f"maxed{c}") for c in range(CHUNKS)]

        mask_go, aggr_go = sem("mask_go"), sem("aggr_go")

        block = stack.enter_context(nc.Block())

        @block.sync
        def _(sp):
            def load_x(n, par):
                sp.dma_start(xT_s[par][:], xT[n]).then_inc(x_in[par], 16)
                sp.dma_start(x_s[par][:], x[n]).then_inc(x_in[par], 16)

            def load_kv(n, par):
                for s in range(GH):
                    sp.dma_start(keys[par][SLOT * s:SLOT * s + HD, s::GH, :], ctxK[n, s]).then_inc(kv_in[par], 16)
                sp.dma_start(vals[par][:], ctxV[n]).then_inc(kv_in[par], 16)

            def halves(w):
                return w.rearrange("(g p) n -> p g n", p=128)

            sp.dma_start(wq_s[:], halves(w_q)).then_inc(in_fold, 16)
            sp.dma_start(dft_s[:], halves(dft)).then_inc(in_fold, 16)
            sp.dma_start(wkv_s[:], halves(w_kv)).then_inc(in_fold, 16)
            load_x(0, 0)
            sp.dma_start(upto_s[:], upto).then_inc(in_const, 16)
            sp.dma_start(mask_s[:], maskneg).then_inc(in_const, 16)
            sp.dma_start(ident_s[:], ident).then_inc(in_const, 16)
            sp.dma_start(woT_s[:], halves(w_oT)).then_inc(in_out, 16)
            sp.dma_start(idftT_s[:], halves(idftT)).then_inc(in_out, 16)
            load_x(1, 1)
            sp.wait_ge(slots_ready, 1)
            load_kv(0, 0)
            sp.dma_start(fw_s[:], halves(ffn_wT)).then_inc(in_ffn, 16)
            sp.dma_start(fv_s[:], halves(ffn_vT)).then_inc(in_ffn, 16)

            def step(t, A, S, F):
                if A and S:
                    sp.wait_ge(pv_done[CHUNKS - 1], t.done(0))
                    load_kv(t.batch(1), 1 - t.par)
                if t.b is None or 0 <= t.b < BATCH - 2:
                    if t.b is None and t.odd:
                        pass
                    sp.wait_ge(proj, t.done(1))
                    sp.wait_ge(added[0], t.done(1))
                    load_x(t.batch(2), t.par)
                if F:
                    sp.wait_ge(out_ready, t.done(0))
                    sp.dma_start(out[t.batch(-1)], res[1 - t.par][:]).then_inc(stored[1 - t.par], 16)

            step(Step(sp, 0), True, True, False)
            with sp.Fori(0, (BATCH - 4) // 2) as pair:
                for odd in range(2):
                    step(Step(sp, None, pair, odd), True, True, True)
            for b in (BATCH - 3, BATCH - 2):
                step(Step(sp, b), True, True, True)
            step(Step(sp, BATCH - 1), False, True, True)
            step(Step(sp, BATCH), False, False, True)
            for i in range(2):
                sp.wait_ge(stored[i], 16 * BATCH // 2)

        @block.gpsimd
        def _(pool):
            pool.wait_ge(zeroed, 1)
            for par in range(2):
                for s in range(GH):
                    last = nc.gpsimd.affine_select(
                        out=keys[par][:, s::GH, :], in_=keys[par][:, s::GH, :], compare_op=ALU.not_equal, fill=1.0,
                        base=-(SLOT * s + HD), pattern=[[0, GROUPS], [0, TOK]], channel_multiplier=1)
            last.then_inc(slots_ready, 1)
            pool.wait_ge(zeroed, 2)

            def step(t, A, S, F):
                if A:
                    pool.wait_ge(approx[CHUNKS - 1], t.done(0))
                    for s in range(GH):
                        pool.dma_start(keys_b[1 - t.par][SLOT * s:SLOT * s + HD, s::GH, :],
                                       ctxK[t.batch(1), s]).then_inc(kb_in[1 - t.par], 16)
                if S:
                    for c in range(CHUNKS):
                        pool.wait_ge(exps[c], t.done(1))
                        pool.sem_inc(mask_go, 1)
                        part = probs[:, GH * c:GH * (c + 1), :]
                        nc.gpsimd.affine_select(out=part, in_=part, compare_op=ALU.is_ge, fill=0.0, base=0,
                                                pattern=[[0, GH], [1, TOK]],
                                                channel_multiplier=-1).then_inc(masked[c], 1)

            steps(pool, step)

        @block.tensor
        def _(pe):
            pe.wait_ge(in_fold, 48)
            for g, dst in enumerate((p_proj[:], p_sum[:].rearrange("p a b -> p (a b)"))):
                for k, w in enumerate((wq_s, wkv_s)):
                    for o in range(2):
                        last = nc.tensor.matmul(dst[:, k * DIM:(k + 1) * DIM], w[:, o, g * 128:(g + 1) * 128],
                                                dft_s[:, o, :], start=(o == 0), stop=(o == 1))
                last.then_inc(folded, 1)
            pe.wait_ge(in_out, 32)
            for g in range(2):
                for o in range(2):
                    last = nc.tensor.matmul(p_tr[:, 2 * g:2 * g + 2, :].rearrange("p a b -> p (a b)"),
                                            idftT_s[:, o, g * 128:(g + 1) * 128], woT_s[:, o, :],
                                            start=(o == 0), stop=(o == 1))
            last.then_inc(folded, 1)
            pe.wait_ge(w_in_ready, 2)
            pe.wait_ge(w_out_ready, 1)
            pe.wait_ge(in_const, 48)
            pe.wait_ge(const_b, 2)

            def project(par, g):
                return nc.tensor.matmul(p_proj[:], xT_s[par][:, g, :], w_in[:, g, :], start=(g == 0), stop=(g == 1))

            def score(t, c):
                for h in range(GH * c, GH * (c + 1)):
                    last = nc.tensor.matmul(p_st[c % 2][:, (h % GH) * TOK:(h % GH + 1) * TOK],
                                            keys[t.par][:, h, :],
                                            x1T[:, h // GH, :], start=True, stop=True)
                last.then_inc(scored[c], 1)

            def weigh(t, c):
                for h in range(GH * c, GH * (c + 1)):
                    last = nc.tensor.matmul(pv[:, h, :], probs[:, h, :], vals[t.par][:, h, :], start=True, stop=True)
                last.then_inc(pv_done[c], 1)

            def step(t, A, S, F):
                new = 1 - t.par
                if A:
                    pe.wait_ge(x_in[new], t.filled(1, 2))
                    pe.wait_ge(normed, t.done(1))
                    pe.wait_ge(added[2], t.done(-1))
                    project(new, 0)
                if S:
                    pe.wait_ge(maxed[CHUNKS - 1], t.done(1))
                    for g in range(GROUPS):
                        last = nc.tensor.transpose(p_tr[:, g, :],
                                                   x1[t.par][:, GH * g:GH * (g + 1), :].rearrange("p h s -> p (h s)"),
                                                   ident_s[:])
                    last.then_inc(x1T_done, 1)
                if A:
                    project(new, 1).then_inc(proj, 1)
                if S:
                    pe.wait_ge(x1T_copied, t.done(1))
                    pe.wait_ge(kv_in[t.par], t.filled(0, GH + 1))
                    pe.wait_ge(exps[2], t.done(0))
                    score(t, 0)
                    pe.wait_ge(exps[3], t.done(0))
                    score(t, 1)
                if A:
                    pe.wait_ge(normed, t.done(2))
                    pe.wait_ge(added[0], t.done(1))
                    nc.tensor.matmul(p_sum[:, 0, :], upto_s[:], unit[:, 1, :, :].rearrange("p k h -> p (k h)"),
                                     start=True, stop=True).then_inc(cum, 1)
                if S:
                    pe.wait_ge(exps[0], t.done(1))
                    score(t, 2)
                if F:
                    pe.wait_ge(xq_done, t.done(0))
                    for g in range(2):
                        last = nc.tensor.transpose(p_trb[:, g, :], xq[:, g * 128:(g + 1) * 128], ident_b[:])
                    last.then_inc(xqT, 1)
                if S:
                    pe.wait_ge(masked[0], t.done(1))
                    pe.wait_ge(att_done, t.done(0))
                    weigh(t, 0)
                    pe.wait_ge(exps[1], t.done(1))
                    score(t, 3)
                if A:
                    pe.wait_ge(y_done, t.done(2))
                    for g in range(2):
                        last = nc.tensor.transpose(p_sum[:, 1, g * TOK:(g + 1) * TOK],
                                                   y[:, g, :, :].rearrange("p k h -> p (k h)"), ident_s[:])
                    last.then_inc(yT, 1)
                if S:
                    pe.wait_ge(masked[1], t.done(1))
                    weigh(t, 1)
                if A:
                    pe.wait_ge(yT_copied, t.done(2))
                    for g in range(2):
                        last = nc.tensor.matmul(p_sum[:, 0, :], yT_s[:, g, :], w_out[:, g, :],
                                                start=(g == 0), stop=(g == 1))
                    last.then_inc(outA, 1)
                if S:
                    pe.wait_ge(masked[2], t.done(1))
                    weigh(t, 2)
                    pe.wait_ge(masked[3], t.done(1))
                    weigh(t, 3)
                if F:
                    pe.wait_ge(xqT_copied, t.done(0))
                if A:
                    pe.wait_ge(x1_b_done, t.done(2))
                    for g in range(GROUPS):
                        last = nc.tensor.transpose(p_trb[:, g, :],
                                                   x1_b[:, GH * g:GH * (g + 1), :].rearrange("p h s -> p (h s)"),
                                                   ident_b[:])
                    last.then_inc(x1T_b_done, 1)
                if F:
                    pe.wait_ge(ffn_seq, 10)
                    for g in range(2):
                        for i in range(3):
                            last = nc.tensor.matmul(p_proj[:, 0:DIM], xqT_s[:, g, :], w_ffn[i][:, g, :],
                                                    start=(g == 0 and i == 0), stop=(g == 1 and i == 2))
                    last.then_inc(ffn, 1)
                if A:
                    pe.wait_ge(x1T_b_copied, t.done(2))
                    pe.wait_ge(kb_in[new], t.filled(1, GH))
                    for c in range(CHUNKS):
                        if c >= 2:
                            pe.wait_ge(maxed[c - 2], t.done(2))
                        nc.tensor.matmul(p_ap[c % 2][:].rearrange("p (h k) -> p h k", h=GH), ident_b[:],
                                         mask_b[:].unsqueeze(1).to_broadcast([128, GH, TOK]), start=True, stop=False)
                        nc.tensor.matmul(p_ap[c % 2][:], x1T_b[:, c, :],
                                         keys_b[new][:, GH * c:GH * (c + 1), :].rearrange("p h k -> p (h k)"),
                                         start=False, stop=True).then_inc(approx[c], 1)

            steps(pe, step)

        @block.scalar
        def _(act):
            for g, src in enumerate((p_proj[:], p_sum[:].rearrange("p a b -> p (a b)"))):
                act.wait_ge(folded, g + 1)
                nc.scalar.activation(w_in[:, g, :], src, ACT.Copy).then_inc(w_in_ready, 1)

            def rsqrt(i, value):
                act.wait_ge(var[i], value)
                nc.scalar.activation(lnv[i][:], mv[i][:, 1:2], ACT.Ln, bias=eps[:]).then_inc(ln_done[i], 1)
                act.wait_ge(ln_done[i], value)
                nc.scalar.activation(rs0[i][:], lnv[i][:], ACT.Exp, scale=-0.5).then_inc(rs_done[i], 1)

            def exponentials(t, c):
                act.wait_ge(scored[c], t.done(1))
                act.wait_ge(pv_done[c], t.done(0))
                nc.scalar.activation(probs[:, GH * c:GH * (c + 1), :].rearrange("p h q -> p (h q)"), p_st[c % 2][:],
                                     ACT.Exp, scale=HD ** -0.5).then_inc(exps[c], 1)

            def step(t, A, S, F):
                if S:
                    act.wait_ge(scored[3], t.done(0))
                    act.wait_ge(x1T_done, t.done(1))
                    nc.scalar.activation(x1T[:], p_tr[:], ACT.Copy).then_inc(x1T_copied, 1)
                if A:
                    act.wait_ge(ssq_done, t.done(1))
                    act.wait_ge(proj, t.done(2))
                    nc.scalar.activation(sq[:], p_proj[:], ACT.Square).then_inc(squared, 1)
                if F:
                    rsqrt(1, t.done(0))
                if S:
                    exponentials(t, 0)
                if A:
                    act.wait_ge(ssq_done, t.done(2))
                    nc.scalar.activation(lnA[:], ssq[:], ACT.Ln).then_inc(lnA_done, 1)
                    act.wait_ge(lnA_done, t.done(2))
                    nc.scalar.activation(rsA[:], lnA[:], ACT.Exp, scale=-0.5).then_inc(rsA_done, 1)
                if S:
                    exponentials(t, 1)
                    exponentials(t, 2)
                if F:
                    act.wait_ge(ffn, t.done(-1))
                    act.wait_ge(xqT, t.done(0))
                    nc.scalar.activation(xqT_s[:], p_trb[:, 0:2, :], ACT.Copy).then_inc(xqT_copied, 1)
                if S:
                    exponentials(t, 3)
                if A:
                    act.wait_ge(outA, t.done(1))
                    act.wait_ge(yT, t.done(2))
                    nc.scalar.activation(yT_s[:], p_sum[:, 1, :].rearrange("p (g q) -> p g q", g=2),
                                         ACT.Copy).then_inc(yT_copied, 1)
                    rsqrt(0, t.done(2))
                    act.wait_ge(x1T_b_done, t.done(1))
                    act.wait_ge(x1_done, t.done(2))
                    nc.scalar.activation(x1_b[:, :, 0:HD], x1[1 - t.par][:, :, 0:HD], ACT.Copy).then_inc(x1_b_done, 1)
                    act.wait_ge(approx[3], t.done(1))
                    act.wait_ge(x1T_b_done, t.done(2))
                    nc.scalar.activation(x1T_b[:], p_trb, ACT.Copy).then_inc(x1T_b_copied, 1)
                if F:
                    rsqrt(2, t.done(0))
                    act.wait_ge(shift_done, t.done(0))
                    if t.b is None or t.b >= 3:
                        act.wait_ge(stored[1 - t.par], t.filled(-3, 1))
                    nc.scalar.activation(res[1 - t.par][:], r3[:], ACT.Identity, bias=shift3[:],
                                         scale=rstd[2][:]).then_inc(out_ready, 1)

            steps(act, step)

        @block.vector
        def _(dve):
            for par in range(2):
                nc.vector.memset(keys[par][:], 0.0)
            nc.vector.memset(eps[:], LN_EPS).then_inc(zeroed, 1)
            for par in range(2):
                nc.vector.memset(keys_b[par][:], 0.0)
                nc.vector.memset(x1[par][:], 0.0)
            nc.vector.memset(x1_b[:], 0.0).then_inc(zeroed, 1)
            dve.wait_ge(in_const, 48)
            nc.vector.tensor_copy(mask_b[:], mask_s[:]).then_inc(const_b, 1)
            nc.vector.tensor_copy(ident_b[:], ident_s[:]).then_inc(const_b, 1)
            dve.wait_ge(folded, 3)
            nc.vector.tensor_copy(w_out[:], p_tr[:].rearrange("p (g a) b -> p g (a b)", g=2)).then_inc(w_out_ready, 1)

            def ffn_weights():
                n = [0]

                def then(ins):
                    n[0] += 1
                    ins.then_inc(ffn_seq, 1)
                    dve.wait_ge(ffn_seq, n[0])

                dve.wait_ge(in_ffn, 32)
                then(nc.vector.tensor_scalar(fa[:], fw_s[:], TH_W, SC_W, ALU.is_gt, ALU.mult))
                then(nc.vector.tensor_scalar(fb[:], fw_s[:], -TH_W, SC_W, ALU.is_lt, ALU.mult))
                then(nc.vector.tensor_tensor(fa[:], fa[:], fb[:], ALU.subtract))
                then(nc.vector.tensor_tensor(fa[:], fa[:], fv_s[:], ALU.add))
                then(nc.vector.tensor_scalar(fb[:], fa[:], -0.5, None, ALU.mult))
                then(nc.vector.tensor_copy(w_ffn[0][:], fb[:]))
                then(nc.vector.tensor_tensor(fa[:], fb[:], w_ffn[0][:], ALU.subtract))
                then(nc.vector.tensor_copy(w_ffn[1][:], fa[:]))
                then(nc.vector.tensor_tensor(fb[:], fa[:], w_ffn[1][:], ALU.subtract))
                then(nc.vector.tensor_copy(w_ffn[2][:], fb[:]))

            def moments(i, r, value):
                dve.wait_ge(added[i], value)
                nc.vector.bn_stats(st[i][:], r[:]).then_inc(stats[i], 1)
                dve.wait_ge(stats[i], value)
                dve.sem_inc(aggr_go, 1)
                nc.vector.bn_aggr(mv[i][:], st[i][:]).then_inc(var[i], 1)

            def newton1(i, value):
                dve.wait_ge(rs_done[i], value)
                nc.vector.scalar_tensor_tensor(out=nt[i][:], in0=rs0[i][:], scalar=-0.5, in1=rs0[i][:],
                                               op0=ALU.mult, op1=ALU.mult).then_inc(nt1[i], 1)

            def newton2(i, value):
                dve.wait_ge(nt1[i], value)
                nc.vector.scalar_tensor_tensor(out=nt[i][:], in0=mv[i][:, 1:2], scalar=LN_EPS, in1=nt[i][:],
                                               op0=ALU.add, op1=ALU.mult).then_inc(nt2[i], 1)

            def newton3(i, value):
                dve.wait_ge(nt2[i], value)
                nc.vector.scalar_tensor_tensor(out=rstd[i][:], in0=nt[i][:], scalar=1.5, in1=rs0[i][:],
                                               op0=ALU.add, op1=ALU.mult).then_inc(rstd_done[i], 1)

            def row_max(t, c):
                dve.wait_ge(approx[c], t.done(2))
                nc.vector.tensor_reduce(x1[1 - t.par][:, GH * c:GH * (c + 1), HD],
                                        p_ap[c % 2][:].rearrange("p (h k) -> p h k", h=GH), AX.X, ALU.max,
                                        negate=True).then_inc(maxed[c], 1)

            def step(t, A, S, F):
                new = 1 - t.par
                if F:
                    dve.wait_ge(pv_done[3], t.done(0))
                    nc.vector.reciprocal(rden[:], pv[:, :, HD]).then_inc(rden_done, 1)
                    dve.wait_ge(rden_done, t.done(0))
                    nc.vector.tensor_tensor(att[:].rearrange("p (h d) -> p h d", h=HEADS), pv[:, :, 0:HD],
                                            rden[:].unsqueeze(2).to_broadcast([128, HEADS, HD]),
                                            ALU.mult).then_inc(att_done, 1)
                    dve.wait_ge(att_done, t.done(0))
                    nc.vector.tensor_tensor(r2[:].rearrange("p (h d) -> p h d", h=HEADS),
                                            att[:].rearrange("p (h d) -> p h d", h=HEADS),
                                            x1[new][:, :, 0:HD], ALU.add).then_inc(added[1], 1)
                    moments(1, r2, t.done(0))
                if A:
                    dve.wait_ge(squared, t.done(2))
                    nc.vector.tensor_reduce(ssq[:].rearrange("p (j h) -> p j h", j=2),
                                            sq[:].rearrange("p (j k h) -> p j h k", j=2, h=HEADS),
                                            AX.X, ALU.add).then_inc(ssq_done, 1)
                if F:
                    newton1(1, t.done(0))
                    newton2(1, t.done(0))
                    newton3(1, t.done(0))
                    dve.wait_ge(rstd_done[1], t.done(0))
                    nc.vector.tensor_scalar(x2[:], r2[:], mv[1][:, 0:1], rstd[1][:], ALU.subtract,
                                            ALU.mult).then_inc(x2_done, 1)
                    dve.wait_ge(x2_done, t.done(0))
                    nc.vector.tensor_scalar(above[:], x2[:], TH_X, None, ALU.is_gt).then_inc(above_done, 1)
                    dve.wait_ge(above_done, t.done(0))
                    dve.wait_ge(xqT, t.done(-1))
                    nc.vector.scalar_tensor_tensor(out=xq[:], in0=x2[:], scalar=-TH_X, in1=above[:],
                                                   op0=ALU.is_lt, op1=ALU.subtract).then_inc(xq_done, 1)
                if A:
                    dve.wait_ge(rsA_done, t.done(2))
                    nc.vector.scalar_tensor_tensor(out=nA[:], in0=rsA[:], scalar=-0.5, in1=rsA[:], op0=ALU.mult,
                                                   op1=ALU.mult).then_inc(nA1, 1)
                    dve.wait_ge(nA1, t.done(2))
                    nc.vector.tensor_tensor(nA[:], nA[:], ssq[:], ALU.mult).then_inc(nA2, 1)
                    dve.wait_ge(nA2, t.done(2))
                    nc.vector.scalar_tensor_tensor(out=rnA[:], in0=nA[:], scalar=1.5, in1=rsA[:], op0=ALU.add,
                                                   op1=ALU.mult).then_inc(rnA_done, 1)
                    dve.wait_ge(rnA_done, t.done(2))
                    dve.wait_ge(cum, t.done(1))
                    nc.vector.tensor_tensor(unit[:], p_proj[:].rearrange("p (j k h) -> p j k h", j=2, h=HEADS),
                                            rnA[:].rearrange("p (j h) -> p j h", j=2).unsqueeze(2)
                                            .to_broadcast([128, 2, 2 * BINS, HEADS]), ALU.mult).then_inc(normed, 1)
                if A:
                    q_s = unit[:, 0, :, :].rearrange("p (i k) h -> p i k h", i=2)
                    kv_s = p_sum[:, 0, :].rearrange("p (i k h) -> p i k h", i=2, h=HEADS)
                    dve.wait_ge(cum, t.done(2))
                    dve.wait_ge(yT, t.done(1))
                    nc.vector.tensor_tensor(y[:], q_s, kv_s, ALU.mult).then_inc(straight, 1)
                    nc.vector.tensor_tensor(cross[:], q_s[:, :, 1:, :], kv_s[:, ::-1, 1:, :],
                                            ALU.mult).then_inc(crossed, 1)
                    dve.wait_ge(straight, t.done(2))
                    nc.vector.tensor_tensor(y[:, 0, 1:, :], y[:, 0, 1:, :], y[:, 1, 1:, :],
                                            ALU.subtract).then_inc(y_cos, 1)
                    dve.wait_ge(crossed, t.done(2))
                    dve.wait_ge(y_cos, t.done(2))
                    nc.vector.tensor_tensor(y[:, 1, 1:, :], cross[:, 0, :, :], cross[:, 1, :, :],
                                            ALU.add).then_inc(y_done, 1)
                    dve.wait_ge(outA, t.done(2))
                    nc.vector.tensor_tensor(r1[:], x_s[new][:], p_sum[:, 0, :], ALU.add).then_inc(added[0], 1)
                    moments(0, r1, t.done(2))
                    newton1(0, t.done(2))
                    newton2(0, t.done(2))
                    newton3(0, t.done(2))
                    dve.wait_ge(rstd_done[0], t.done(2))
                    dve.wait_ge(x1T_done, t.done(0))
                    nc.vector.tensor_scalar(x1[new][:, :, 0:HD], r1[:].rearrange("p (h d) -> p h d", h=HEADS),
                                            mv[0][:, 0:1], rstd[0][:], ALU.subtract, ALU.mult).then_inc(x1_done, 1)
                if t.b == 0:
                    ffn_weights()
                if F:
                    dve.wait_ge(ffn, t.done(0))
                    dve.wait_ge(out_ready, t.done(-1))
                    nc.vector.tensor_tensor(r3[:], x2[:], p_proj[:, 0:DIM], ALU.add).then_inc(added[2], 1)
                    moments(2, r3, t.done(0))
                if A:
                    row_max(t, 0)
                if F:
                    newton1(2, t.done(0))
                if A:
                    row_max(t, 1)
                if F:
                    newton2(2, t.done(0))
                if A:
                    row_max(t, 2)
                if F:
                    newton3(2, t.done(0))
                if A:
                    row_max(t, 3)
                if F:
                    dve.wait_ge(rstd_done[2], t.done(0))
                    nc.vector.scalar_tensor_tensor(out=shift3[:], in0=mv[2][:, 0:1], scalar=-1.0, in1=rstd[2][:],
                                                   op0=ALU.mult, op1=ALU.mult).then_inc(shift_done, 1)

            steps(dve, step)


def dft_tables():
    import numpy as np

    n = np.arange(HD)
    fwd = np.zeros((HEADS, HD, 2, BINS, HEADS))
    inv = np.zeros((HEADS, HD, 2, BINS, HEADS))
    for k in range(BINS):
        for half in range(2):
            if k == 0:
                row, gain = ((-1.0) ** (n * half)) / HD ** 0.5, HD ** 0.5 / HD
            else:
                angle = 2 * np.pi * k * n / HD
                row, gain = (np.sin if half else np.cos)(angle) * (2 / HD) ** 0.5, (HD / 2) ** 0.5 / HD
            for h in range(HEADS):
                fwd[h, :, half, k, h] = row
                inv[h, :, half, k, h] = row * gain
    return (fwd.reshape(DIM, DIM).astype(np.float32), inv.reshape(DIM, DIM).astype(np.float32))


def kernel(x, ctx_2048, L0_attn_W_q, L0_attn_W_kv, L0_attn_W_o, L0_ffn_weight, L0_ffn_rram_variation):
    import numpy as np
    import concourse.bacc as bacc
    from concourse.bass_utils import run_bass_kernel_spmd

    x, ctx = np.asarray(x), np.asarray(ctx_2048)
    fwd, inv = dft_tables()
    tok = np.arange(TOK)
    vals = np.ones((BATCH, TOK, HEADS, VW), np.float32)
    vals[..., :HD] = ctx.reshape(BATCH, TOK, HEADS, HD)
    arrays = {
        "x": x,
        "xT": x.reshape(BATCH, TOK, 2, 128).transpose(0, 3, 2, 1),
        "ctxK": ctx.reshape(BATCH, TOK, GROUPS, GH, HD).transpose(0, 3, 4, 2, 1),
        "ctxV": vals,
        "w_q": L0_attn_W_q,
        "w_kv": L0_attn_W_kv,
        "w_oT": np.asarray(L0_attn_W_o).T,
        "ffn_wT": np.asarray(L0_ffn_weight).T,
        "ffn_vT": np.asarray(L0_ffn_rram_variation).T,
        "dft": fwd,
        "idftT": inv,
        "upto": (tok[:, None] <= tok[None, :]).astype(np.float32),
        "maskneg": np.where(tok[None, :] <= tok[:, None], 0.0, MASK).astype(np.float32),
        "ident": np.eye(128, dtype=np.float32),
    }
    arrays = {n: np.ascontiguousarray(a) for n, a in arrays.items()}
    nc = bacc.Bacc("TRN2", target_bir_lowering=False, num_devices=1)
    args = [nc.dram_tensor(n, a.shape, mybir.dt.from_np(a.dtype), kind="ExternalInput").ap() for n, a in arrays.items()]
    out = nc.dram_tensor("out", (BATCH, TOK, DIM), mybir.dt.float32, kind="ExternalOutput").ap()
    decoder_layer(nc, *args, out)
    r = run_bass_kernel_spmd(nc, [arrays], core_ids=[0])
    return r.results[0]["out"]
```

```python
import concourse.bass as bass
from concourse import mybir
from contextlib import ExitStack

BATCH, TOK, DIM, HEADS = 16, 128, 256, 16
HD = DIM // HEADS
BINS = HD // 2
HALF = DIM // 2
SLOT = 32
GROUPS = HEADS * SLOT // 128
GH = HEADS // GROUPS
CHUNKS = GROUPS
CW = GH * TOK
LN_EPS = 1e-5
TH_X, TH_W, SC_W = 0.33, 0.2, 0.6
MASK = -1e30


class Step:

    def __init__(self, eng, b=None, pair=None, odd=0):
        self.eng, self.b, self.pair, self.odd, self.held = eng, b, pair, odd, {}
        self.par = (b if b is not None else odd) % 2

    def done(self, off):
        if self.b is not None:
            return max(0, self.b + off)
        if off not in self.held:
            self.held[off] = self.eng.snap(2 * self.pair + (2 + self.odd + off))
        return self.held[off]

    def filled(self, off, dmas):
        if self.b is not None:
            return 16 * dmas * ((self.b + off) // 2 + 1)
        key = (off, dmas)
        if key not in self.held:
            self.held[key] = self.eng.snap(16 * dmas * self.pair + 16 * dmas * ((2 + self.odd + off) // 2 + 1))
        return self.held[key]

    def batch(self, off):
        return self.b + off if self.b is not None else 2 * self.pair + (2 + self.odd + off)


def steps(eng, step):
    step(Step(eng, -2), True, False, False, False)
    step(Step(eng, -1), True, True, False, False)
    step(Step(eng, 0), True, True, True, False)
    step(Step(eng, 1), True, True, True, True)
    with eng.Fori(0, (BATCH - 4) // 2) as pair:
        for odd in range(2):
            step(Step(eng, None, pair, odd), True, True, True, True)
    step(Step(eng, BATCH - 2), False, True, True, True)
    step(Step(eng, BATCH - 1), False, False, True, True)
    step(Step(eng, BATCH), False, False, False, True)


def decoder_layer(nc, x, xT, ctxK, ctxV, w_q, w_kv, w_oT, ffn_wT, ffn_vT, dft, idftT, upto, maskneg, ident, out):
    f32, bf16 = mybir.dt.float32, mybir.dt.bfloat16
    ALU, ACT, AX = mybir.AluOpType, mybir.ActivationFunctionType, mybir.AxisListType

    with ExitStack() as stack:
        def sb(name, shape, dt=f32):
            return stack.enter_context(nc.sbuf_tensor(name, shape, dt))

        def bank(name, shape, dt=f32):
            return stack.enter_context(nc.psum_tensor(name, shape, dt))

        def sem(name):
            return stack.enter_context(nc.semaphore(name))

        wq_s, wkv_s, woT_s = (sb(n, [128, 2, DIM]) for n in ("wq_s", "wkv_s", "woT_s"))
        dft_s, idftT_s = sb("dft_s", [128, 2, DIM]), sb("idftT_s", [128, 2, DIM])
        upto_s, mask_s, ident_s = sb("upto_s", [128, TOK]), sb("mask_s", [128, TOK]), sb("ident_s", [128, 128])
        mask_b, ident_b = sb("mask_b", [128, TOK], bf16), sb("ident_b", [128, 128], bf16)
        w_in = sb("w_in", [128, 2, 2 * DIM])
        w_out = sb("w_out", [128, 2, DIM])
        fw_s, fv_s = sb("fw_s", [128, 2, DIM]), sb("fv_s", [128, 2, DIM])
        fa, fb = sb("fa", [128, 2, DIM]), sb("fb", [128, 2, DIM])
        w_ffn = [sb(f"w_ffn{i}", [128, 2, DIM], bf16) for i in range(3)]

        x_s = [sb(f"x_s{i}", [128, DIM]) for i in range(2)]
        xT_s = [sb(f"xT_s{i}", [128, 2, TOK]) for i in range(2)]
        keys = [sb(f"keys{i}", [128, HEADS, TOK]) for i in range(2)]
        keys_b = [sb(f"keys_b{i}", [128, HEADS, TOK], bf16) for i in range(2)]
        vals = [sb(f"vals{i}", [128, HEADS, SLOT]) for i in range(2)]

        sq = sb("sq", [128, 2 * DIM])
        ssq, lnA, rsA, nA, rnA = (sb(n, [128, 2 * HEADS]) for n in ("ssq", "lnA", "rsA", "nA", "rnA"))
        unit = sb("unit", [128, 2, 2 * BINS, HEADS])
        y = sb("y", [128, 2, BINS, HEADS])
        cross = sb("cross", [128, 2, BINS - 1, HEADS])
        yT_s = sb("yT_s", [128, 2, TOK])
        r1, r2, r3 = sb("r1", [128, DIM]), sb("r2", [128, DIM]), sb("r3", [128, DIM])
        x1 = [sb(f"x1_{i}", [128, HEADS, SLOT]) for i in range(2)]
        x1_b = sb("x1_b", [128, HEADS, SLOT], bf16)
        x1T_b = sb("x1T_b", [128, GROUPS, TOK], bf16)
        x1T = sb("x1T", [128, GROUPS, TOK])
        probs = sb("probs", [128, HEADS, TOK])
        outT_s = sb("outT_s", [128, GROUPS, TOK])
        rden = sb("rden", [128, HEADS])
        att = sb("att", [128, DIM])
        x2 = sb("x2", [128, DIM])
        above, xq = sb("above", [128, DIM], bf16), sb("xq", [128, DIM], bf16)
        xqT_s = sb("xqT_s", [128, 2, TOK], bf16)
        res = [sb(f"res{i}", [128, DIM]) for i in range(2)]
        st = [sb(f"st{i}", [128, 6]) for i in range(3)]
        mv = [sb(f"mv{i}", [128, 2]) for i in range(3)]
        lnv, rs0, nt, rstd = ([sb(f"{n}{i}", [128, 1]) for i in range(3)] for n in ("lnv", "rs0", "nt", "rstd"))
        shift3 = sb("shift3", [128, 1])
        eps = sb("eps", [128, 1])

        p_proj = bank("p_proj", [128, 2 * DIM])
        p_sum = bank("p_sum", [128, 2, DIM])
        p_tr = bank("p_tr", [128, GROUPS, TOK])
        p_out = bank("p_out", [128, GROUPS, TOK])
        p_st = [bank(f"p_st{i}", [128, CW]) for i in range(2)]
        p_ap = [bank(f"p_ap{i}", [128, CW]) for i in range(2)]
        p_trb = p_tr[:].rearrange("p a b -> p (a b)").bitcast(bf16)[:, 0:CW].rearrange("p (a b) -> p a b", a=GROUPS)
        pv = p_st[1][:].rearrange("p (h w) -> p h w", h=HEADS)

        in_fold, in_out, in_const, in_ffn = (sem(n) for n in ("in_fold", "in_out", "in_const", "in_ffn"))
        x_in = [sem(f"x_in{i}") for i in range(2)]
        kv_in = [sem(f"kv_in{i}") for i in range(2)]
        kb_in = [sem(f"kb_in{i}") for i in range(2)]
        stored = [sem(f"stored{i}") for i in range(2)]
        zeroed, slots_ready, folded, w_in_ready, w_out_ready, const_b, ffn_seq = (
            sem(n) for n in ("zeroed", "slots_ready", "folded", "w_in_ready", "w_out_ready", "const_b", "ffn_seq"))
        (proj, cum, yT, outA, x1T_b_done, x1T_done, xqT, ffn, out_done) = (
            sem(n) for n in ("proj", "cum", "yT", "outA", "x1T_b_done", "x1T_done", "xqT", "ffn", "out_done"))
        approx = [sem(f"approx{c}") for c in range(CHUNKS)]
        scored = [sem(f"scored{c}") for c in range(CHUNKS)]
        pv_done = [sem(f"pv_done{c}") for c in range(CHUNKS)]
        (squared, lnA_done, rsA_done, yT_copied, x1_b_done, x1T_b_copied, x1T_copied, xqT_copied, outT_copied,
         out_ready) = (
            sem(n) for n in ("squared", "lnA_done", "rsA_done", "yT_copied", "x1_b_done", "x1T_b_copied",
                             "x1T_copied", "xqT_copied", "outT_copied", "out_ready"))
        ln_done = [sem(f"ln_done{i}") for i in range(3)]
        rs_done = [sem(f"rs_done{i}") for i in range(3)]
        exps = [sem(f"exps{c}") for c in range(CHUNKS)]
        masked = [sem(f"masked{c}") for c in range(CHUNKS)]
        (ssq_done, nA1, nA2, rnA_done, normed, straight, crossed, y_cos, y_done, shift_done, rden_done, att_done,
         x1_done, x2_done, above_done, xq_done) = (
            sem(n) for n in ("ssq_done", "nA1", "nA2", "rnA_done", "normed", "straight", "crossed", "y_cos",
                             "y_done", "shift_done", "rden_done", "att_done", "x1_done", "x2_done",
                             "above_done", "xq_done"))
        added, stats, var, nt1, nt2, rstd_done = ([sem(f"{n}{i}") for i in range(3)]
                                                  for n in ("added", "stats", "var", "nt1_", "nt2_", "rstd_done"))
        maxed = [sem(f"maxed{c}") for c in range(CHUNKS)]

        mask_go, aggr_go = sem("mask_go"), sem("aggr_go")

        block = stack.enter_context(nc.Block())

        @block.sync
        def _(sp):
            def load_x(n, par):
                sp.dma_start(xT_s[par][:], xT[n]).then_inc(x_in[par], 16)
                sp.dma_start(x_s[par][:], x[n]).then_inc(x_in[par], 16)

            def load_kv(n, par):
                for s in range(GH):
                    sp.dma_start(keys[par][SLOT * s:SLOT * s + HD, s::GH, :], ctxK[n, s]).then_inc(kv_in[par], 16)
                sp.dma_start(vals[par][:], ctxV[n]).then_inc(kv_in[par], 16)

            def halves(w):
                return w.rearrange("(g p) n -> p g n", p=128)

            sp.dma_start(wq_s[:], halves(w_q)).then_inc(in_fold, 16)
            sp.dma_start(dft_s[:], halves(dft)).then_inc(in_fold, 16)
            sp.dma_start(wkv_s[:], halves(w_kv)).then_inc(in_fold, 16)
            load_x(0, 0)
            sp.dma_start(upto_s[:], upto).then_inc(in_const, 16)
            sp.dma_start(mask_s[:], maskneg).then_inc(in_const, 16)
            sp.dma_start(ident_s[:], ident).then_inc(in_const, 16)
            sp.dma_start(woT_s[:], halves(w_oT)).then_inc(in_out, 16)
            sp.dma_start(idftT_s[:], halves(idftT)).then_inc(in_out, 16)
            load_x(1, 1)
            for i in range(2):
                sp.sem_inc(stored[i], 16)
            sp.wait_ge(slots_ready, 1)
            load_kv(0, 0)
            sp.dma_start(fw_s[:], halves(ffn_wT)).then_inc(in_ffn, 16)
            sp.dma_start(fv_s[:], halves(ffn_vT)).then_inc(in_ffn, 16)

            def load_and_store(t, x_too, kv_too, store):
                if kv_too:
                    sp.wait_ge(pv_done[CHUNKS - 1], t.done(0))
                    load_kv(t.batch(1), 1 - t.par)
                if x_too:
                    sp.wait_ge(proj, t.done(2))
                    sp.wait_ge(added[0], t.done(2))
                    load_x(t.batch(3), 1 - t.par)
                if store:
                    sp.wait_ge(out_ready, t.done(0))
                    sp.dma_start(out[t.batch(-1)], res[1 - t.par][:]).then_inc(stored[1 - t.par], 16)

            load_and_store(Step(sp, -1), True, False, False)
            load_and_store(Step(sp, 0), True, True, False)
            load_and_store(Step(sp, 1), True, True, True)
            with sp.Fori(0, (BATCH - 6) // 2) as pair:
                for odd in range(2):
                    load_and_store(Step(sp, None, pair, odd), True, True, True)
            for b in range(BATCH - 4, BATCH + 1):
                load_and_store(Step(sp, b), b + 3 < BATCH, b + 1 < BATCH, True)
            for i in range(2):
                sp.wait_ge(stored[i], 16 * (BATCH // 2 + 1))

        @block.gpsimd
        def _(pool):
            pool.wait_ge(zeroed, 1)
            for par in range(2):
                for s in range(GH):
                    last = nc.gpsimd.affine_select(
                        out=keys[par][:, s::GH, :], in_=keys[par][:, s::GH, :], compare_op=ALU.not_equal, fill=1.0,
                        base=-(SLOT * s + HD), pattern=[[0, GROUPS], [0, TOK]], channel_multiplier=1)
            last.then_inc(slots_ready, 1)
            pool.wait_ge(zeroed, 2)

            def step(t, P, A, S, F):
                if A:
                    pool.wait_ge(approx[CHUNKS - 1], t.done(0))
                    for s in range(GH):
                        pool.dma_start(keys_b[1 - t.par][SLOT * s:SLOT * s + HD, s::GH, :],
                                       ctxK[t.batch(1), s]).then_inc(kb_in[1 - t.par], 16)
                if S:
                    for c in range(CHUNKS):
                        pool.wait_ge(exps[c], t.done(1))
                        pool.sem_inc(mask_go, 1)
                        part = probs[:, GH * c:GH * (c + 1), :]
                        nc.gpsimd.affine_select(out=part, in_=part, compare_op=ALU.is_ge, fill=0.0, base=0,
                                                pattern=[[0, GH], [1, TOK]],
                                                channel_multiplier=-1).then_inc(masked[c], 1)

            steps(pool, step)

        @block.tensor
        def _(pe):
            pe.wait_ge(in_fold, 48)
            for g, dst in enumerate((p_proj[:], p_sum[:].rearrange("p a b -> p (a b)"))):
                for k, w in enumerate((wq_s, wkv_s)):
                    for o in range(2):
                        last = nc.tensor.matmul(dst[:, k * DIM:(k + 1) * DIM], w[:, o, g * 128:(g + 1) * 128],
                                                dft_s[:, o, :], start=(o == 0), stop=(o == 1))
                last.then_inc(folded, 1)
            pe.wait_ge(in_out, 32)
            for g in range(2):
                for o in range(2):
                    last = nc.tensor.matmul(p_tr[:, 2 * g:2 * g + 2, :].rearrange("p a b -> p (a b)"),
                                            idftT_s[:, o, g * 128:(g + 1) * 128], woT_s[:, o, :],
                                            start=(o == 0), stop=(o == 1))
            last.then_inc(folded, 1)
            pe.wait_ge(w_in_ready, 2)
            pe.wait_ge(w_out_ready, 1)
            pe.wait_ge(in_const, 48)
            pe.wait_ge(const_b, 2)

            def score(t, c):
                for h in range(GH * c, GH * (c + 1)):
                    last = nc.tensor.matmul(p_st[c % 2][:, (h % GH) * TOK:(h % GH + 1) * TOK],
                                            keys[t.par][:, h, :],
                                            x1T[:, h // GH, :], start=True, stop=True)
                last.then_inc(scored[c], 1)

            def weigh(t, c):
                for j in range(GH):
                    h = GH * c + j
                    last = nc.tensor.matmul(p_out[SLOT * j:SLOT * (j + 1), c, :], vals[t.par][:, h, :], probs[:, h, :],
                                            start=True, stop=True)
                last.then_inc(pv_done[c], 1)

            def approximate(t, c):
                nc.tensor.matmul(p_ap[c % 2][:].rearrange("p (h k) -> p h k", h=GH), ident_b[:],
                                 mask_b[:].unsqueeze(1).to_broadcast([128, GH, TOK]), start=True, stop=False)
                nc.tensor.matmul(p_ap[c % 2][:], x1T_b[:, c, :],
                                 keys_b[1 - t.par][:, GH * c:GH * (c + 1), :].rearrange("p h k -> p (h k)"),
                                 start=False, stop=True).then_inc(approx[c], 1)

            def step(t, P, A, S, F):
                if S:
                    pe.wait_ge(maxed[CHUNKS - 1], t.done(1))
                    for g in range(GROUPS):
                        last = nc.tensor.transpose(p_tr[:, g, :],
                                                   x1[t.par][:, GH * g:GH * (g + 1), :].rearrange("p h s -> p (h s)"),
                                                   ident_s[:])
                    last.then_inc(x1T_done, 1)
                if A:
                    pe.wait_ge(normed, t.done(2))
                    pe.wait_ge(added[0], t.done(1))
                    nc.tensor.matmul(p_sum[:, 0, :], upto_s[:], unit[:, 1, :, :].rearrange("p k h -> p (k h)"),
                                     start=True, stop=True).then_inc(cum, 1)
                if S:
                    pe.wait_ge(x1T_copied, t.done(1))
                    pe.wait_ge(kv_in[t.par], t.filled(0, GH + 1))
                    pe.wait_ge(exps[2], t.done(0))
                    score(t, 0)
                    pe.wait_ge(att_done, t.done(0))
                    score(t, 1)
                if A:
                    pe.wait_ge(y_done, t.done(2))
                    for g in range(2):
                        last = nc.tensor.transpose(p_sum[:, 1, g * TOK:(g + 1) * TOK],
                                                   y[:, g, :, :].rearrange("p k h -> p (k h)"), ident_s[:])
                    last.then_inc(yT, 1)
                if S:
                    pe.wait_ge(exps[0], t.done(1))
                    score(t, 2)
                if A:
                    pe.wait_ge(yT_copied, t.done(2))
                    for g in range(2):
                        last = nc.tensor.matmul(p_sum[:, 0, :], yT_s[:, g, :], w_out[:, g, :],
                                                start=(g == 0), stop=(g == 1))
                    last.then_inc(outA, 1)
                if P:
                    pe.wait_ge(x_in[t.par], t.filled(2, 2))
                    pe.wait_ge(normed, t.done(2))
                    for g in range(2):
                        last = nc.tensor.matmul(p_proj[:], xT_s[t.par][:, g, :], w_in[:, g, :],
                                                start=(g == 0), stop=(g == 1))
                    last.then_inc(proj, 1)
                if F:
                    pe.wait_ge(xq_done, t.done(0))
                    for g in range(2):
                        last = nc.tensor.transpose(p_trb[:, g, :], xq[:, g * 128:(g + 1) * 128], ident_b[:])
                    last.then_inc(xqT, 1)
                if S:
                    pe.wait_ge(masked[0], t.done(1))
                    pe.wait_ge(outT_copied, t.done(0))
                    weigh(t, 0)
                    pe.wait_ge(exps[1], t.done(1))
                    score(t, 3)
                if F:
                    pe.wait_ge(xqT_copied, t.done(0))
                if A:
                    pe.wait_ge(x1_b_done, t.done(2))
                    for g in range(GROUPS):
                        last = nc.tensor.transpose(p_trb[:, g, :],
                                                   x1_b[:, GH * g:GH * (g + 1), :].rearrange("p h s -> p (h s)"),
                                                   ident_b[:])
                    last.then_inc(x1T_b_done, 1)
                if S:
                    pe.wait_ge(masked[1], t.done(1))
                    weigh(t, 1)
                if A:
                    pe.wait_ge(x1T_b_copied, t.done(2))
                    pe.wait_ge(kb_in[1 - t.par], t.filled(1, GH))
                    approximate(t, 0)
                if F:
                    if A:
                        pe.wait_ge(added[0], t.done(2))
                    pe.wait_ge(ffn_seq, 10)
                    for g in range(2):
                        for i in range(3):
                            last = nc.tensor.matmul(p_sum[:, 1, :], xqT_s[:, g, :], w_ffn[i][:, g, :],
                                                    start=(g == 0 and i == 0), stop=(g == 1 and i == 2))
                    last.then_inc(ffn, 1)
                if A:
                    approximate(t, 1)
                if S:
                    pe.wait_ge(masked[2], t.done(1))
                    weigh(t, 2)
                if A:
                    pe.wait_ge(maxed[0], t.done(2))
                    approximate(t, 2)
                if S:
                    pe.wait_ge(masked[3], t.done(1))
                    weigh(t, 3)
                if A:
                    pe.wait_ge(maxed[1], t.done(2))
                    approximate(t, 3)
                if S:
                    pe.wait_ge(outT_copied, t.done(1))
                    for g in range(GROUPS):
                        last = nc.tensor.transpose(p_st[1][:, g * 128:(g + 1) * 128], outT_s[:, g, :], ident_s[:])
                    last.then_inc(out_done, 1)

            steps(pe, step)

        @block.scalar
        def _(act):
            act.preload_act_table_set("natural_log_exp_and_others")
            for g, src in enumerate((p_proj[:], p_sum[:].rearrange("p a b -> p (a b)"))):
                act.wait_ge(folded, g + 1)
                nc.scalar.activation(w_in[:, g, :], src, ACT.Copy).then_inc(w_in_ready, 1)

            def rsqrt(i, value):
                act.wait_ge(var[i], value)
                nc.scalar.activation(lnv[i][:], mv[i][:, 1:2], ACT.Ln, bias=eps[:]).then_inc(ln_done[i], 1)
                act.wait_ge(ln_done[i], value)
                nc.scalar.activation(rs0[i][:], lnv[i][:], ACT.Exp, scale=-0.5).then_inc(rs_done[i], 1)

            def exponentials(t, c):
                act.wait_ge(scored[c], t.done(1))
                act.wait_ge(pv_done[c], t.done(0))
                nc.scalar.activation(probs[:, GH * c:GH * (c + 1), :].rearrange("p h q -> p (h q)"), p_st[c % 2][:],
                                     ACT.Exp, scale=HD ** -0.5).then_inc(exps[c], 1)

            def step(t, P, A, S, F):
                if S:
                    act.wait_ge(scored[3], t.done(0))
                    act.wait_ge(x1T_done, t.done(1))
                    nc.scalar.activation(x1T[:], p_tr[:], ACT.Copy).then_inc(x1T_copied, 1)
                    exponentials(t, 0)
                    exponentials(t, 1)
                if A:
                    act.wait_ge(outA, t.done(1))
                    act.wait_ge(yT, t.done(2))
                    nc.scalar.activation(yT_s[:], p_sum[:, 1, :].rearrange("p (g q) -> p g q", g=2),
                                         ACT.Copy).then_inc(yT_copied, 1)
                if F:
                    rsqrt(1, t.done(0))
                if S:
                    exponentials(t, 2)
                if A:
                    rsqrt(0, t.done(2))
                if P:
                    act.wait_ge(ssq_done, t.done(2))
                    act.wait_ge(proj, t.done(3))
                    nc.scalar.activation(sq[:], p_proj[:], ACT.Square).then_inc(squared, 1)
                if F:
                    act.wait_ge(xqT, t.done(0))
                    nc.scalar.activation(xqT_s[:], p_trb[:, 0:2, :], ACT.Copy).then_inc(xqT_copied, 1)
                if A:
                    act.wait_ge(x1T_b_done, t.done(1))
                    act.wait_ge(x1_done, t.done(2))
                    nc.scalar.activation(x1_b[:, :, 0:HD], x1[1 - t.par][:, :, 0:HD], ACT.Copy).then_inc(x1_b_done, 1)
                if P:
                    act.wait_ge(ssq_done, t.done(3))
                    nc.scalar.activation(lnA[:], ssq[:], ACT.Ln).then_inc(lnA_done, 1)
                    act.wait_ge(lnA_done, t.done(3))
                    nc.scalar.activation(rsA[:], lnA[:], ACT.Exp, scale=-0.5).then_inc(rsA_done, 1)
                if S:
                    exponentials(t, 3)
                if A:
                    act.wait_ge(approx[3], t.done(1))
                    act.wait_ge(x1T_b_done, t.done(2))
                    nc.scalar.activation(x1T_b[:], p_trb, ACT.Copy).then_inc(x1T_b_copied, 1)
                if F:
                    rsqrt(2, t.done(0))
                    act.wait_ge(shift_done, t.done(0))
                    act.wait_ge(stored[1 - t.par], t.filled(-1, 1))
                    nc.scalar.activation(res[1 - t.par][:], r3[:], ACT.Identity, bias=shift3[:],
                                         scale=rstd[2][:]).then_inc(out_ready, 1)
                if S:
                    act.wait_ge(out_done, t.done(0))
                    act.wait_ge(pv_done[3], t.done(1))
                    nc.scalar.activation(outT_s[:], p_out[:], ACT.Copy).then_inc(outT_copied, 1)

            steps(act, step)

        @block.vector
        def _(dve):
            for par in range(2):
                nc.vector.memset(keys[par][:], 0.0)
            nc.vector.memset(eps[:], LN_EPS).then_inc(zeroed, 1)
            for par in range(2):
                nc.vector.memset(keys_b[par][:], 0.0)
                nc.vector.memset(x1[par][:], 0.0)
            nc.vector.memset(x1_b[:], 0.0).then_inc(zeroed, 1)
            dve.wait_ge(in_const, 48)
            nc.vector.tensor_copy(mask_b[:], mask_s[:]).then_inc(const_b, 1)
            nc.vector.tensor_copy(ident_b[:], ident_s[:]).then_inc(const_b, 1)
            dve.wait_ge(folded, 3)
            nc.vector.tensor_copy(w_out[:], p_tr[:].rearrange("p (g a) b -> p g (a b)", g=2)).then_inc(w_out_ready, 1)

            def ffn_weights():
                n = [0]

                def then(ins):
                    n[0] += 1
                    ins.then_inc(ffn_seq, 1)
                    dve.wait_ge(ffn_seq, n[0])

                dve.wait_ge(in_ffn, 32)
                then(nc.vector.tensor_scalar(fa[:], fw_s[:], TH_W, SC_W, ALU.is_gt, ALU.mult))
                then(nc.vector.tensor_scalar(fb[:], fw_s[:], -TH_W, SC_W, ALU.is_lt, ALU.mult))
                then(nc.vector.tensor_tensor(fa[:], fa[:], fb[:], ALU.subtract))
                then(nc.vector.tensor_tensor(fa[:], fa[:], fv_s[:], ALU.add))
                then(nc.vector.tensor_scalar(fb[:], fa[:], -0.5, None, ALU.mult))
                then(nc.vector.tensor_copy(w_ffn[0][:], fb[:]))
                then(nc.vector.tensor_tensor(fa[:], fb[:], w_ffn[0][:], ALU.subtract))
                then(nc.vector.tensor_copy(w_ffn[1][:], fa[:]))
                then(nc.vector.tensor_tensor(fb[:], fa[:], w_ffn[1][:], ALU.subtract))
                then(nc.vector.tensor_copy(w_ffn[2][:], fb[:]))

            def moments(i, r, value):
                dve.wait_ge(added[i], value)
                nc.vector.bn_stats(st[i][:], r[:]).then_inc(stats[i], 1)
                dve.wait_ge(stats[i], value)
                dve.sem_inc(aggr_go, 1)
                nc.vector.bn_aggr(mv[i][:], st[i][:]).then_inc(var[i], 1)

            def newton1(i, value):
                dve.wait_ge(rs_done[i], value)
                nc.vector.scalar_tensor_tensor(out=nt[i][:], in0=rs0[i][:], scalar=-0.5, in1=rs0[i][:],
                                               op0=ALU.mult, op1=ALU.mult).then_inc(nt1[i], 1)

            def newton2(i, value):
                dve.wait_ge(nt1[i], value)
                nc.vector.scalar_tensor_tensor(out=nt[i][:], in0=mv[i][:, 1:2], scalar=LN_EPS, in1=nt[i][:],
                                               op0=ALU.add, op1=ALU.mult).then_inc(nt2[i], 1)

            def newton3(i, value):
                dve.wait_ge(nt2[i], value)
                nc.vector.scalar_tensor_tensor(out=rstd[i][:], in0=nt[i][:], scalar=1.5, in1=rs0[i][:],
                                               op0=ALU.add, op1=ALU.mult).then_inc(rstd_done[i], 1)

            def row_max(t, c):
                dve.wait_ge(approx[c], t.done(2))
                nc.vector.tensor_reduce(x1[1 - t.par][:, GH * c:GH * (c + 1), HD],
                                        p_ap[c % 2][:].rearrange("p (h k) -> p h k", h=GH), AX.X, ALU.max,
                                        negate=True).then_inc(maxed[c], 1)

            def step(t, P, A, S, F):
                new = 1 - t.par
                if F:
                    dve.wait_ge(out_done, t.done(0))
                    nc.vector.reciprocal(rden[:], pv[:, :, HD]).then_inc(rden_done, 1)
                    dve.wait_ge(rden_done, t.done(0))
                    nc.vector.tensor_tensor(att[:].rearrange("p (h d) -> p h d", h=HEADS), pv[:, :, 0:HD],
                                            rden[:].unsqueeze(2).to_broadcast([128, HEADS, HD]),
                                            ALU.mult).then_inc(att_done, 1)
                if A:
                    q_s = unit[:, 0, :, :].rearrange("p (i k) h -> p i k h", i=2)
                    kv_s = p_sum[:, 0, :].rearrange("p (i k h) -> p i k h", i=2, h=HEADS)
                    dve.wait_ge(cum, t.done(2))
                    dve.wait_ge(yT, t.done(1))
                    nc.vector.tensor_tensor(y[:], q_s, kv_s, ALU.mult).then_inc(straight, 1)
                    nc.vector.tensor_tensor(cross[:], q_s[:, :, 1:, :], kv_s[:, ::-1, 1:, :],
                                            ALU.mult).then_inc(crossed, 1)
                    dve.wait_ge(straight, t.done(2))
                    nc.vector.tensor_tensor(y[:, 0, 1:, :], y[:, 0, 1:, :], y[:, 1, 1:, :],
                                            ALU.subtract).then_inc(y_cos, 1)
                    dve.wait_ge(crossed, t.done(2))
                    dve.wait_ge(y_cos, t.done(2))
                    nc.vector.tensor_tensor(y[:, 1, 1:, :], cross[:, 0, :, :], cross[:, 1, :, :],
                                            ALU.add).then_inc(y_done, 1)
                if F:
                    dve.wait_ge(att_done, t.done(0))
                    nc.vector.tensor_tensor(r2[:].rearrange("p (h d) -> p h d", h=HEADS),
                                            att[:].rearrange("p (h d) -> p h d", h=HEADS),
                                            x1[new][:, :, 0:HD], ALU.add).then_inc(added[1], 1)
                    moments(1, r2, t.done(0))
                    newton1(1, t.done(0))
                    newton2(1, t.done(0))
                    newton3(1, t.done(0))
                    dve.wait_ge(rstd_done[1], t.done(0))
                    nc.vector.tensor_scalar(x2[:], r2[:], mv[1][:, 0:1], rstd[1][:], ALU.subtract,
                                            ALU.mult).then_inc(x2_done, 1)
                    dve.wait_ge(x2_done, t.done(0))
                    nc.vector.tensor_scalar(above[:], x2[:], TH_X, None, ALU.is_gt).then_inc(above_done, 1)
                    dve.wait_ge(above_done, t.done(0))
                    nc.vector.scalar_tensor_tensor(out=xq[:], in0=x2[:], scalar=-TH_X, in1=above[:],
                                                   op0=ALU.is_lt, op1=ALU.subtract).then_inc(xq_done, 1)
                if A:
                    dve.wait_ge(outA, t.done(2))
                    nc.vector.tensor_tensor(r1[:], x_s[new][:], p_sum[:, 0, :], ALU.add).then_inc(added[0], 1)
                    moments(0, r1, t.done(2))
                    newton1(0, t.done(2))
                    newton2(0, t.done(2))
                    newton3(0, t.done(2))
                    dve.wait_ge(rstd_done[0], t.done(2))
                    dve.wait_ge(x1T_done, t.done(0))
                    nc.vector.tensor_scalar(x1[new][:, :, 0:HD], r1[:].rearrange("p (h d) -> p h d", h=HEADS),
                                            mv[0][:, 0:1], rstd[0][:], ALU.subtract, ALU.mult).then_inc(x1_done, 1)
                if P:
                    dve.wait_ge(squared, t.done(3))
                    nc.vector.tensor_reduce(ssq[:].rearrange("p (j h) -> p j h", j=2),
                                            sq[:].rearrange("p (j k h) -> p j h k", j=2, h=HEADS),
                                            AX.X, ALU.add).then_inc(ssq_done, 1)
                    dve.wait_ge(rsA_done, t.done(3))
                    nc.vector.scalar_tensor_tensor(out=nA[:], in0=rsA[:], scalar=-0.5, in1=rsA[:], op0=ALU.mult,
                                                   op1=ALU.mult).then_inc(nA1, 1)
                    dve.wait_ge(nA1, t.done(3))
                    nc.vector.tensor_tensor(nA[:], nA[:], ssq[:], ALU.mult).then_inc(nA2, 1)
                    dve.wait_ge(nA2, t.done(3))
                    nc.vector.scalar_tensor_tensor(out=rnA[:], in0=nA[:], scalar=1.5, in1=rsA[:], op0=ALU.add,
                                                   op1=ALU.mult).then_inc(rnA_done, 1)
                    dve.wait_ge(rnA_done, t.done(3))
                    dve.wait_ge(y_done, t.done(2))
                    nc.vector.tensor_tensor(unit[:], p_proj[:].rearrange("p (j k h) -> p j k h", j=2, h=HEADS),
                                            rnA[:].rearrange("p (j h) -> p j h", j=2).unsqueeze(2)
                                            .to_broadcast([128, 2, 2 * BINS, HEADS]), ALU.mult).then_inc(normed, 1)
                if t.b == 0:
                    ffn_weights()
                if A:
                    row_max(t, 0)
                if F:
                    dve.wait_ge(ffn, t.done(0))
                    nc.vector.tensor_tensor(r3[:], x2[:], p_sum[:, 1, :], ALU.add).then_inc(added[2], 1)
                    moments(2, r3, t.done(0))
                if A:
                    row_max(t, 1)
                if F:
                    newton1(2, t.done(0))
                    newton2(2, t.done(0))
                if A:
                    row_max(t, 2)
                if F:
                    newton3(2, t.done(0))
                    dve.wait_ge(rstd_done[2], t.done(0))
                    nc.vector.scalar_tensor_tensor(out=shift3[:], in0=mv[2][:, 0:1], scalar=-1.0, in1=rstd[2][:],
                                                   op0=ALU.mult, op1=ALU.mult).then_inc(shift_done, 1)
                if A:
                    row_max(t, 3)

            steps(dve, step)


def dft_tables():
    import numpy as np

    n = np.arange(HD)
    fwd = np.zeros((HEADS, HD, 2, BINS, HEADS))
    inv = np.zeros((HEADS, HD, 2, BINS, HEADS))
    for k in range(BINS):
        for half in range(2):
            if k == 0:
                row, gain = ((-1.0) ** (n * half)) / HD ** 0.5, HD ** 0.5 / HD
            else:
                angle = 2 * np.pi * k * n / HD
                row, gain = (np.sin if half else np.cos)(angle) * (2 / HD) ** 0.5, (HD / 2) ** 0.5 / HD
            for h in range(HEADS):
                fwd[h, :, half, k, h] = row
                inv[h, :, half, k, h] = row * gain
    return (fwd.reshape(DIM, DIM).astype(np.float32), inv.reshape(DIM, DIM).astype(np.float32))


def kernel(x, ctx_2048, L0_attn_W_q, L0_attn_W_kv, L0_attn_W_o, L0_ffn_weight, L0_ffn_rram_variation):
    import numpy as np
    import concourse.bacc as bacc
    from concourse.bass_utils import run_bass_kernel_spmd

    x, ctx = np.asarray(x), np.asarray(ctx_2048)
    fwd, inv = dft_tables()
    tok = np.arange(TOK)
    vals = np.zeros((BATCH, TOK, HEADS, SLOT), np.float32)
    vals[..., :HD] = ctx.reshape(BATCH, TOK, HEADS, HD)
    vals[..., HD] = 1.0
    arrays = {
        "x": x,
        "xT": x.reshape(BATCH, TOK, 2, 128).transpose(0, 3, 2, 1),
        "ctxK": ctx.reshape(BATCH, TOK, GROUPS, GH, HD).transpose(0, 3, 4, 2, 1),
        "ctxV": vals,
        "w_q": L0_attn_W_q,
        "w_kv": L0_attn_W_kv,
        "w_oT": np.asarray(L0_attn_W_o).T,
        "ffn_wT": np.asarray(L0_ffn_weight).T,
        "ffn_vT": np.asarray(L0_ffn_rram_variation).T,
        "dft": fwd,
        "idftT": inv,
        "upto": (tok[:, None] <= tok[None, :]).astype(np.float32),
        "maskneg": np.where(tok[None, :] <= tok[:, None], 0.0, MASK).astype(np.float32),
        "ident": np.eye(128, dtype=np.float32),
    }
    arrays = {n: np.ascontiguousarray(a) for n, a in arrays.items()}
    nc = bacc.Bacc("TRN2", target_bir_lowering=False, num_devices=1)
    args = [nc.dram_tensor(n, a.shape, mybir.dt.from_np(a.dtype), kind="ExternalInput").ap() for n, a in arrays.items()]
    out = nc.dram_tensor("out", (BATCH, TOK, DIM), mybir.dt.float32, kind="ExternalOutput").ap()
    decoder_layer(nc, *args, out)
    r = run_bass_kernel_spmd(nc, [arrays], core_ids=[0])
    return r.results[0]["out"]
```

```python
import concourse.bass as bass
from concourse import mybir
from contextlib import ExitStack

BATCH, TOK, DIM, HEADS = 16, 128, 256, 16
HD = DIM // HEADS
BINS = HD // 2
SLOT = 32
GROUPS = HEADS * SLOT // 128
GH = HEADS // GROUPS
CHUNKS = GROUPS
CW = GH * TOK
LN_EPS = 1e-5
TH_X, TH_W, SC_W = 0.33, 0.2, 0.6
FIRST, FAR, NEAR = 1e20, 1e17, 1e-4


class Step:

    def __init__(self, eng, b=None, trip=None, unroll=4, first=0):
        self.eng, self.b, self.trip, self.unroll, self.held = eng, b, trip, unroll, {}
        self.at = first if b is None else b
        self.par = self.at % 2

    def batch(self, off):
        return self.b + off if self.b is not None else self.unroll * self.trip + (self.at + off)

    def done(self, off):
        if self.b is not None:
            return max(0, self.b + off)
        if off not in self.held:
            self.held[off] = self.eng.snap(self.batch(off))
        return self.held[off]

    def filled(self, off, dmas, bufs=2):
        turns = (self.at + off) // bufs + 1
        if self.b is not None:
            return 16 * dmas * turns
        if (off, dmas) not in self.held:
            self.held[off, dmas] = self.eng.snap(16 * dmas * self.unroll // bufs * self.trip + 16 * dmas * turns)
        return self.held[off, dmas]

    def has(self, off):
        return self.b is None or 0 <= self.b + off < BATCH


def steps(eng, step):
    for b in range(-3, 1):
        step(Step(eng, b))
    with eng.Fori(0, (BATCH - 4) // 4) as trip:
        for k in range(4):
            step(Step(eng, None, trip, 4, 1 + k))
    for b in range(BATCH - 3, BATCH + 1):
        step(Step(eng, b))


def decoder_layer(nc, x, xT, ctxK, ctxV, w_q, w_kv, w_oT, ffn_wT, ffn_vT, dft, idftT, upto, pairs, barred, ident, out):
    f32, bf16 = mybir.dt.float32, mybir.dt.bfloat16
    ALU, ACT, AX = mybir.AluOpType, mybir.ActivationFunctionType, mybir.AxisListType

    with ExitStack() as stack:
        def sb(name, shape, dt=f32):
            return stack.enter_context(nc.sbuf_tensor(name, shape, dt))

        def bank(name, shape, dt=f32):
            return stack.enter_context(nc.psum_tensor(name, shape, dt))

        def sem(name):
            return stack.enter_context(nc.semaphore(name))

        wq_s, wkv_s, woT_s = (sb(n, [128, 2, DIM]) for n in ("wq_s", "wkv_s", "woT_s"))
        dft_s, idftT_s = sb("dft_s", [128, 2, DIM]), sb("idftT_s", [128, 2, DIM])
        upto_s, ident_s = sb("upto_s", [128, TOK]), sb("ident_s", [128, 128])
        pairs_s, barred_s = sb("pairs_s", [128, GH, SLOT - HD]), sb("barred_s", [128, TOK])
        ident_b = sb("ident_b", [128, 128], bf16)
        w_in = sb("w_in", [128, 2, 2 * DIM])
        w_out = sb("w_out", [128, 2, DIM])
        fw_s, fv_s = sb("fw_s", [128, 2, DIM]), sb("fv_s", [128, 2, DIM])
        fa, fb = sb("fa", [128, 2, DIM]), sb("fb", [128, 2, DIM])
        w_ffn = [sb(f"w_ffn{i}", [128, 2, DIM], bf16) for i in range(3)]

        x_s = [sb(f"x_s{i}", [128, DIM]) for i in range(4)]
        xT_s = [sb(f"xT_s{i}", [128, 2, TOK]) for i in range(4)]
        keys = [sb(f"keys{i}", [128, HEADS, TOK]) for i in range(4)]
        keys_b = [sb(f"keys_b{i}", [128, HEADS, TOK], bf16) for i in range(2)]
        vals = [sb(f"vals{i}", [128, HEADS, SLOT]) for i in range(4)]

        sq = sb("sq", [128, 2 * DIM])
        ssq, lnA, rsA, nA, rnA = (sb(n, [128, 2 * HEADS]) for n in ("ssq", "lnA", "rsA", "nA", "rnA"))
        unit = sb("unit", [128, 2, 2 * BINS, HEADS])
        y = sb("y", [128, 2, BINS, HEADS])
        cross = sb("cross", [128, 2, BINS - 1, HEADS])
        yT_s = sb("yT_s", [128, 2, TOK])
        r1, r2, r3 = sb("r1", [128, DIM]), sb("r2", [128, DIM]), sb("r3", [128, DIM])
        x1 = [sb(f"x1_{i}", [128, HEADS, SLOT]) for i in range(4)]
        x1_b = sb("x1_b", [128, HEADS, SLOT], bf16)
        x1T_b = sb("x1T_b", [128, GROUPS, TOK], bf16)
        x1T = sb("x1T", [128, GROUPS, TOK])
        probs = sb("probs", [128, HEADS, TOK])
        outT_s = sb("outT_s", [128, GROUPS, TOK])
        rden = sb("rden", [128, HEADS])
        att = sb("att", [128, DIM])
        x2 = sb("x2", [128, DIM])
        above, xq = sb("above", [128, DIM], bf16), sb("xq", [128, DIM], bf16)
        xqT_s = sb("xqT_s", [128, 2, TOK], bf16)
        res = [sb(f"res{i}", [128, DIM]) for i in range(2)]
        st = [sb(f"st{i}", [128, 6]) for i in range(3)]
        mv = [sb(f"mv{i}", [128, 2]) for i in range(3)]
        lnv, rs0, nt, rstd = ([sb(f"{n}{i}", [128, 1]) for i in range(3)] for n in ("lnv", "rs0", "nt", "rstd"))
        shift3 = sb("shift3", [128, 1])
        eps = sb("eps", [128, 1])
        warm = sb("warm", [128, CW], bf16)

        p_proj = bank("p_proj", [128, 2 * DIM])
        p_sum = bank("p_sum", [128, 2, DIM])
        p_tr = bank("p_tr", [128, GROUPS, TOK])
        p_out = bank("p_out", [128, GROUPS, TOK])
        p_st = [bank(f"p_st{i}", [128, CW]) for i in range(2)]
        p_ap = [bank(f"p_ap{i}", [128, CW]) for i in range(2)]
        p_trb = p_tr[:].rearrange("p a b -> p (a b)").bitcast(bf16)[:, 0:CW].rearrange("p (a b) -> p a b", a=GROUPS)
        pv = p_st[1][:].rearrange("p (h w) -> p h w", h=HEADS)

        in_fold, in_fold_kv, in_out, in_const, in_ffn = (
            sem(n) for n in ("in_fold", "in_fold_kv", "in_out", "in_const", "in_ffn"))
        x_in = [sem(f"x_in{i}") for i in range(4)]
        kv_in = [sem(f"kv_in{i}") for i in range(4)]
        stored = [sem(f"stored{i}") for i in range(2)]
        warm_ready, zeroed, slots_ready, folded, w_in_ready, w_out_ready, const_b, ffn_seq = (
            sem(n) for n in ("warm_ready", "zeroed", "slots_ready", "folded", "w_in_ready", "w_out_ready",
                             "const_b", "ffn_seq"))
        (proj, cum, yT, outA, x1T_b_done, x1T_done, xqT, ffn, out_done) = (
            sem(n) for n in ("proj", "cum", "yT", "outA", "x1T_b_done", "x1T_done", "xqT", "ffn", "out_done"))
        approx = [sem(f"approx{c}") for c in range(CHUNKS)]
        scored = [sem(f"scored{c}") for c in range(CHUNKS)]
        pv_done = [sem(f"pv_done{c}") for c in range(CHUNKS)]
        (keys_cast, squared, lnA_done, rsA_done, yT_copied, x1_b_done, x1T_b_copied, x1T_copied, xqT_copied,
         outT_copied, out_ready) = (
            sem(n) for n in ("keys_cast", "squared", "lnA_done", "rsA_done", "yT_copied", "x1_b_done", "x1T_b_copied",
                             "x1T_copied", "xqT_copied", "outT_copied", "out_ready"))
        ln_done = [sem(f"ln_done{i}") for i in range(3)]
        rs_done = [sem(f"rs_done{i}") for i in range(3)]
        exps = [sem(f"exps{c}") for c in range(CHUNKS)]
        masked = [sem(f"masked{c}") for c in range(CHUNKS)]
        (ssq_done, nA1, nA2, rnA_done, normed, straight, crossed, y_cos, y_done, shift_done, rden_done, att_done,
         x1_done, x2_done, above_done, xq_done) = (
            sem(n) for n in ("ssq_done", "nA1", "nA2", "rnA_done", "normed", "straight", "crossed", "y_cos",
                             "y_done", "shift_done", "rden_done", "att_done", "x1_done", "x2_done",
                             "above_done", "xq_done"))
        added, stats, var, nt1, nt2, rstd_done = ([sem(f"{n}{i}") for i in range(3)]
                                                  for n in ("added", "stats", "var", "nt1_", "nt2_", "rstd_done"))
        maxed = [sem(f"maxed{c}") for c in range(CHUNKS)]

        mask_go, aggr_go = sem("mask_go"), sem("aggr_go")

        block = stack.enter_context(nc.Block())

        @block.sync
        def _(sp):
            def load_x(n, buf):
                sp.dma_start(xT_s[buf][:], xT[n]).then_inc(x_in[buf], 16)
                sp.dma_start(x_s[buf][:], x[n]).then_inc(x_in[buf], 16)

            def load_kv(n, buf):
                for s in range(GH):
                    sp.dma_start(keys[buf][SLOT * s:SLOT * s + HD, s::GH, :], ctxK[n, s]).then_inc(kv_in[buf], 16)
                sp.dma_start(vals[buf][:], ctxV[n]).then_inc(kv_in[buf], 16)

            def halves(w):
                return w.rearrange("(g p) n -> p g n", p=128)

            sp.dma_start(wq_s[:], halves(w_q)).then_inc(in_fold, 16)
            sp.dma_start(dft_s[:], halves(dft)).then_inc(in_fold, 16)
            sp.dma_start(wkv_s[:], halves(w_kv)).then_inc(in_fold_kv, 16)
            load_x(0, 0)
            sp.dma_start(woT_s[:], halves(w_oT)).then_inc(in_out, 16)
            sp.dma_start(idftT_s[:], halves(idftT)).then_inc(in_out, 16)
            sp.dma_start(upto_s[:], upto).then_inc(in_const, 16)
            sp.dma_start(pairs_s[:], pairs).then_inc(in_const, 16)
            sp.dma_start(barred_s[:], barred).then_inc(in_const, 16)
            sp.dma_start(ident_s[:], ident).then_inc(in_const, 16)
            load_x(1, 1)
            load_x(2, 2)
            for i in range(2):
                sp.sem_inc(stored[i], 16)
            sp.wait_ge(slots_ready, 1)
            load_kv(0, 0)
            sp.dma_start(fw_s[:], halves(ffn_wT)).then_inc(in_ffn, 16)
            sp.dma_start(fv_s[:], halves(ffn_vT)).then_inc(in_ffn, 16)
            for n in range(1, 3):
                sp.wait_ge(slots_ready, n + 1)
                load_kv(n, n)
            load_x(3, 3)
            sp.wait_ge(slots_ready, 4)

            def load_and_store(t, x_too, kv_too, store):
                if kv_too:
                    if t.b != 0:
                        sp.wait_ge(pv_done[CHUNKS - 1], t.done(0))
                    load_kv(t.batch(3), (t.at + 3) % 4)
                if x_too:
                    sp.wait_ge(proj, t.done(1))
                    sp.wait_ge(added[0], t.done(1))
                    load_x(t.batch(4), t.at % 4)
                if store:
                    sp.wait_ge(out_ready, t.done(0))
                    sp.dma_start(out[t.batch(-1)], res[1 - t.par][:]).then_inc(stored[1 - t.par], 16)

            load_and_store(Step(sp, 0), True, True, False)
            with sp.Fori(0, (BATCH - 5) // 4) as trip:
                for k in range(4):
                    load_and_store(Step(sp, None, trip, 4, 1 + k), True, True, True)
            for b in range((BATCH - 5) // 4 * 4 + 1, BATCH + 1):
                load_and_store(Step(sp, b), b + 4 < BATCH, b + 3 < BATCH, True)
            for i in range(2):
                sp.wait_ge(stored[i], 16 * (BATCH // 2 + 1))

        @block.gpsimd
        def _(pool):
            for n, tile in enumerate(keys):
                if n >= 2:
                    nc.gpsimd.memset(tile[:], 0.0).then_inc(zeroed, 1)
                pool.wait_ge(zeroed, n + 1)
                for s in range(GH):
                    last = nc.gpsimd.affine_select(
                        out=tile[:, s::GH, :], in_=tile[:, s::GH, :], compare_op=ALU.not_equal, fill=1.0,
                        base=-(SLOT * s + HD), pattern=[[0, GROUPS], [0, TOK]], channel_multiplier=1)
                last.then_inc(slots_ready, 1)

            def ffn_weights():
                n = [0]

                def then(ins):
                    n[0] += 1
                    ins.then_inc(ffn_seq, 1)
                    pool.wait_ge(ffn_seq, n[0])

                pool.wait_ge(in_ffn, 32)
                then(nc.gpsimd.tensor_scalar(fa[:], fw_s[:], TH_W, SC_W, ALU.is_gt, ALU.mult))
                then(nc.gpsimd.tensor_scalar(fb[:], fw_s[:], -TH_W, SC_W, ALU.is_lt, ALU.mult))
                then(nc.gpsimd.tensor_tensor(fa[:], fa[:], fb[:], ALU.subtract))
                then(nc.gpsimd.tensor_tensor(fa[:], fa[:], fv_s[:], ALU.add))
                then(nc.gpsimd.tensor_scalar(fb[:], fa[:], -0.5, None, ALU.mult))
                then(nc.gpsimd.tensor_copy(w_ffn[0][:], fb[:]))
                then(nc.gpsimd.tensor_tensor(fa[:], fb[:], w_ffn[0][:], ALU.subtract))
                then(nc.gpsimd.tensor_copy(w_ffn[1][:], fa[:]))
                then(nc.gpsimd.tensor_tensor(fb[:], fa[:], w_ffn[1][:], ALU.subtract))
                then(nc.gpsimd.tensor_copy(w_ffn[2][:], fb[:]))

            def step(t):
                if t.has(0):
                    for c in range(CHUNKS):
                        pool.wait_ge(exps[c], t.done(1))
                        pool.sem_inc(mask_go, 1)
                        part = probs[:, GH * c:GH * (c + 1), :]
                        nc.gpsimd.affine_select(out=part, in_=part, compare_op=ALU.is_ge, fill=0.0, base=0,
                                                pattern=[[0, GH], [1, TOK]],
                                                channel_multiplier=-1).then_inc(masked[c], 1)
                if t.b == -2:
                    ffn_weights()

            steps(pool, step)

        @block.tensor
        def _(pe):
            pe.wait_ge(warm_ready, 1)
            for i in range(7):
                nc.tensor.matmul(p_ap[0][:], warm[:, 0:128], warm[:], start=True, stop=True)
            for k, w in enumerate((wq_s, wkv_s)):
                if k == 0:
                    pe.wait_ge(in_fold, 32)
                else:
                    pe.wait_ge(in_fold_kv, 16)
                for g, dst in enumerate((p_proj[:], p_sum[:].rearrange("p a b -> p (a b)"))):
                    for o in range(2):
                        last = nc.tensor.matmul(dst[:, k * DIM:(k + 1) * DIM], w[:, o, g * 128:(g + 1) * 128],
                                                dft_s[:, o, :], start=(o == 0), stop=(o == 1))
                    if k == 1:
                        last.then_inc(folded, 1)
            pe.wait_ge(in_out, 32)
            for g in range(2):
                for o in range(2):
                    last = nc.tensor.matmul(p_tr[:, 2 * g:2 * g + 2, :].rearrange("p a b -> p (a b)"),
                                            idftT_s[:, o, g * 128:(g + 1) * 128], woT_s[:, o, :],
                                            start=(o == 0), stop=(o == 1))
            last.then_inc(folded, 1)
            pe.wait_ge(w_in_ready, 2)

            def project(bank, buf):
                for g in range(2):
                    last = nc.tensor.matmul(bank[:], xT_s[buf][:, g, :], w_in[:, g, :], start=(g == 0), stop=(g == 1))
                last.then_inc(proj, 1)

            def score(t, c):
                for h in range(GH * c, GH * (c + 1)):
                    last = nc.tensor.matmul(p_st[c % 2][:, (h % GH) * TOK:(h % GH + 1) * TOK],
                                            keys[t.at % 4][:, h, :],
                                            x1T[:, h // GH, :], start=True, stop=True)
                last.then_inc(scored[c], 1)

            def weigh(t, c):
                for j in range(GH):
                    h = GH * c + j
                    last = nc.tensor.matmul(p_out[SLOT * j:SLOT * (j + 1), c, :], vals[t.at % 4][:, h, :],
                                            probs[:, h, :], start=True, stop=True)
                last.then_inc(pv_done[c], 1)

            def approximate(t, c):
                nc.tensor.matmul(p_ap[c % 2][:], x1T_b[:, c, :],
                                 keys_b[1 - t.par][:, GH * c:GH * (c + 1), :].rearrange("p h k -> p (h k)"),
                                 start=True, stop=True).then_inc(approx[c], 1)

            def step(t):
                if t.b == -3:
                    for n, bank in enumerate((p_proj, p_ap[0])):
                        pe.wait_ge(x_in[n], 32)
                        project(bank, n)
                if t.b == -2:
                    pe.wait_ge(x_in[2], 32)
                    pe.wait_ge(normed, 1)
                    project(p_proj, 2)
                    pe.wait_ge(w_out_ready, 1)
                    pe.wait_ge(const_b, 2)
                if t.has(3) and t.b not in (-3, -2, -1):
                    pe.wait_ge(x_in[(t.at + 3) % 4], t.filled(3, 2, 4))
                    pe.wait_ge(normed, t.done(3))
                    pe.wait_ge(added[2], t.done(0))
                    project(p_proj, (t.at + 3) % 4)
                if t.has(1):
                    pe.wait_ge(x1T_copied, t.done(1))
                    pe.wait_ge(x1_b_done, t.done(2))
                    for g in range(GROUPS):
                        last = nc.tensor.transpose(p_trb[:, g, :],
                                                   x1_b[:, GH * g:GH * (g + 1), :].rearrange("p h s -> p (h s)"),
                                                   ident_b[:])
                    last.then_inc(x1T_b_done, 1)
                if t.has(0):
                    pe.wait_ge(x1T_copied, t.done(1))
                    pe.wait_ge(kv_in[t.at % 4], t.filled(0, GH + 1, 4))
                    pe.wait_ge(exps[2], t.done(0))
                    score(t, 0)
                    pe.wait_ge(att_done, t.done(0))
                    score(t, 1)
                if t.has(2):
                    pe.wait_ge(y_done, t.done(3))
                    for g in range(2):
                        last = nc.tensor.transpose(p_sum[:, 1, g * TOK:(g + 1) * TOK],
                                                   y[:, g, :, :].rearrange("p k h -> p (k h)"), ident_s[:])
                    last.then_inc(yT, 1)
                if t.has(1):
                    pe.wait_ge(x1T_b_copied, t.done(2))
                    pe.wait_ge(keys_cast, t.done(2))
                    approximate(t, 0)
                    approximate(t, 1)
                if t.has(0):
                    pe.wait_ge(exps[0], t.done(1))
                    score(t, 2)
                if t.has(2):
                    pe.wait_ge(yT_copied, t.done(3))
                    for g in range(2):
                        last = nc.tensor.matmul(p_sum[:, 0, :], yT_s[:, g, :], w_out[:, g, :],
                                                start=(g == 0), stop=(g == 1))
                    last.then_inc(outA, 1)
                if t.has(1):
                    pe.wait_ge(maxed[0], t.done(2))
                    approximate(t, 2)
                if t.has(-1):
                    pe.wait_ge(xq_done, t.done(0))
                    for g in range(2):
                        last = nc.tensor.transpose(p_trb[:, g, :], xq[:, g * 128:(g + 1) * 128], ident_b[:])
                    last.then_inc(xqT, 1)
                if t.has(0):
                    pe.wait_ge(exps[1], t.done(1))
                    score(t, 3)
                if t.has(-1):
                    if t.has(3):
                        pe.wait_ge(normed, t.done(4))
                    pe.wait_ge(xqT_copied, t.done(0))
                    pe.wait_ge(ffn_seq, 10)
                    for g in range(2):
                        for i in range(3):
                            last = nc.tensor.matmul(p_proj[:, 0:DIM], xqT_s[:, g, :], w_ffn[i][:, g, :],
                                                    start=(g == 0 and i == 0), stop=(g == 1 and i == 2))
                    last.then_inc(ffn, 1)
                if t.has(0):
                    pe.wait_ge(masked[0], t.done(1))
                    pe.wait_ge(outT_copied, t.done(0))
                    weigh(t, 0)
                if t.has(1):
                    pe.wait_ge(maxed[1], t.done(2))
                    approximate(t, 3)
                if t.has(0):
                    pe.wait_ge(masked[1], t.done(1))
                    weigh(t, 1)
                    pe.wait_ge(masked[2], t.done(1))
                    weigh(t, 2)
                    pe.wait_ge(masked[3], t.done(1))
                    weigh(t, 3)
                if t.has(3):
                    pe.wait_ge(normed, t.done(4))
                    pe.wait_ge(added[0], t.done(3))
                    if t.b == -3:
                        pe.wait_ge(in_const, 64)
                    nc.tensor.matmul(p_sum[:, 0, :], upto_s[:], unit[:, 1, :, :].rearrange("p k h -> p (k h)"),
                                     start=True, stop=True).then_inc(cum, 1)
                if t.has(1):
                    pe.wait_ge(maxed[CHUNKS - 1], t.done(2))
                    for g in range(GROUPS):
                        last = nc.tensor.transpose(p_tr[:, g, :],
                                                   x1[(t.at + 1) % 4][:, GH * g:GH * (g + 1), :]
                                                   .rearrange("p h s -> p (h s)"), ident_s[:])
                    last.then_inc(x1T_done, 1)
                if t.has(0):
                    pe.wait_ge(outT_copied, t.done(1))
                    for g in range(GROUPS):
                        last = nc.tensor.transpose(p_st[1][:, g * 128:(g + 1) * 128], outT_s[:, g, :], ident_s[:])
                    last.then_inc(out_done, 1)

            steps(pe, step)

        @block.scalar
        def _(act):
            act.preload_act_table_set("natural_log_exp_and_others")
            for g, src in enumerate((p_proj[:], p_sum[:].rearrange("p a b -> p (a b)"))):
                act.wait_ge(folded, g + 1)
                nc.scalar.activation(w_in[:, g, :], src, ACT.Copy).then_inc(w_in_ready, 1)

            def log_var(i, value):
                act.wait_ge(var[i], value)
                nc.scalar.activation(lnv[i][:], mv[i][:, 1:2], ACT.Ln, bias=eps[:]).then_inc(ln_done[i], 1)

            def rsqrt(i, value):
                act.wait_ge(ln_done[i], value)
                nc.scalar.activation(rs0[i][:], lnv[i][:], ACT.Exp, scale=-0.5).then_inc(rs_done[i], 1)

            def cast_keys(t, s):
                if s == 0:
                    act.wait_ge(kv_in[(t.at + 2) % 4], t.filled(2, GH + 1, 4))
                    act.wait_ge(approx[CHUNKS - 1], t.done(1))
                    if t.b == -2:
                        act.wait_ge(const_b, 2)
                rows = slice(SLOT * s, SLOT * s + HD)
                ins = nc.scalar.activation(keys_b[t.par][rows, s::GH, :], keys[(t.at + 2) % 4][rows, s::GH, :],
                                           ACT.Copy)
                if s == GH - 1:
                    ins.then_inc(keys_cast, 1)

            def exponentials(t, c):
                act.wait_ge(scored[c], t.done(1))
                act.wait_ge(pv_done[c], t.done(0))
                nc.scalar.activation(probs[:, GH * c:GH * (c + 1), :].rearrange("p h q -> p (h q)"), p_st[c % 2][:],
                                     ACT.Exp, scale=HD ** -0.5).then_inc(exps[c], 1)

            def step(t):
                if t.has(2):
                    cast_keys(t, 0)
                if t.has(3):
                    act.wait_ge(ssq_done, t.done(3))
                    act.wait_ge(proj, t.done(4))
                    nc.scalar.activation(sq[:], (p_ap[0] if t.b == -2 else p_proj)[:], ACT.Square).then_inc(squared, 1)
                if t.has(1):
                    act.wait_ge(approx[3], t.done(1))
                    act.wait_ge(x1T_b_done, t.done(2))
                    nc.scalar.activation(x1T_b[:], p_trb, ACT.Copy).then_inc(x1T_b_copied, 1)
                if t.has(-1):
                    log_var(1, t.done(0))
                    rsqrt(1, t.done(0))
                if t.has(0):
                    exponentials(t, 0)
                if t.has(3):
                    act.wait_ge(ssq_done, t.done(4))
                    nc.scalar.activation(lnA[:], ssq[:], ACT.Ln).then_inc(lnA_done, 1)
                if t.has(2):
                    act.wait_ge(outA, t.done(2))
                    act.wait_ge(yT, t.done(3))
                    nc.scalar.activation(yT_s[:], p_sum[:, 1, :].rearrange("p (g q) -> p g q", g=2),
                                         ACT.Copy).then_inc(yT_copied, 1)
                if t.has(3):
                    act.wait_ge(lnA_done, t.done(4))
                    nc.scalar.activation(rsA[:], lnA[:], ACT.Exp, scale=-0.5).then_inc(rsA_done, 1)
                if t.has(0):
                    exponentials(t, 1)
                    exponentials(t, 2)
                if t.has(2):
                    cast_keys(t, 1)
                if t.has(-1):
                    act.wait_ge(xqT, t.done(0))
                    nc.scalar.activation(xqT_s[:], p_trb[:, 0:2, :], ACT.Copy).then_inc(xqT_copied, 1)
                if t.has(2):
                    cast_keys(t, 2)
                if t.has(0):
                    exponentials(t, 3)
                if t.has(2):
                    log_var(0, t.done(3))
                    rsqrt(0, t.done(3))
                if t.has(0):
                    act.wait_ge(out_done, t.done(0))
                    act.wait_ge(pv_done[3], t.done(1))
                    nc.scalar.activation(outT_s[:], p_out[:], ACT.Copy).then_inc(outT_copied, 1)
                if t.has(-1):
                    log_var(2, t.done(0))
                    rsqrt(2, t.done(0))
                if t.has(2):
                    cast_keys(t, 3)
                if t.has(1):
                    act.wait_ge(scored[3], t.done(1))
                    act.wait_ge(x1T_done, t.done(2))
                    nc.scalar.activation(x1T[:], p_tr[:], ACT.Copy).then_inc(x1T_copied, 1)
                if t.has(2):
                    act.wait_ge(x1T_b_done, t.done(2))
                    act.wait_ge(x1_done, t.done(3))
                    nc.scalar.activation(x1_b[:, :, 0:HD], x1[(t.at + 2) % 4][:, :, 0:HD],
                                         ACT.Copy).then_inc(x1_b_done, 1)
                if t.has(-1):
                    act.wait_ge(shift_done, t.done(0))
                    act.wait_ge(stored[1 - t.par], t.filled(-1, 1))
                    nc.scalar.activation(res[1 - t.par][:], r3[:], ACT.Identity, bias=shift3[:],
                                         scale=rstd[2][:]).then_inc(out_ready, 1)

            steps(act, step)

        @block.vector
        def _(dve):
            nc.vector.memset(warm[:], 0.0).then_inc(warm_ready, 1)
            for tile in keys[0:2]:
                nc.vector.memset(tile[:], 0.0).then_inc(zeroed, 1)
            nc.vector.memset(eps[:], LN_EPS)
            for tile in x1:
                nc.vector.memset(tile[:], 0.0)
            dve.sem_inc(added[2], 1)
            dve.wait_ge(in_const, 64)
            for g in range(GROUPS):
                nc.vector.tensor_copy(x1_b[:, GH * g:GH * (g + 1), HD:], pairs_s[:])
            for tile in keys_b:
                last = nc.vector.tensor_copy(tile[:], barred_s[:].unsqueeze(1).to_broadcast([128, HEADS, TOK]))
            last.then_inc(const_b, 1)
            nc.vector.tensor_copy(ident_b[:], ident_s[:]).then_inc(const_b, 1)
            dve.wait_ge(folded, 3)
            nc.vector.tensor_copy(w_out[:], p_tr[:].rearrange("p (g a) b -> p g (a b)", g=2)).then_inc(w_out_ready, 1)

            def statistics(i, r):
                nc.vector.bn_stats(st[i][:], r[:]).then_inc(stats[i], 1)

            def moments(i, value):
                dve.wait_ge(stats[i], value)
                dve.sem_inc(aggr_go, 1)
                nc.vector.bn_aggr(mv[i][:], st[i][:]).then_inc(var[i], 1)

            def newton1(i, value):
                dve.wait_ge(rs_done[i], value)
                nc.vector.scalar_tensor_tensor(out=nt[i][:], in0=rs0[i][:], scalar=-0.5, in1=rs0[i][:],
                                               op0=ALU.mult, op1=ALU.mult).then_inc(nt1[i], 1)

            def newton2(i, value):
                dve.wait_ge(nt1[i], value)
                nc.vector.scalar_tensor_tensor(out=nt[i][:], in0=mv[i][:, 1:2], scalar=LN_EPS, in1=nt[i][:],
                                               op0=ALU.add, op1=ALU.mult).then_inc(nt2[i], 1)

            def newton3(i, value):
                dve.wait_ge(nt2[i], value)
                nc.vector.scalar_tensor_tensor(out=rstd[i][:], in0=nt[i][:], scalar=1.5, in1=rs0[i][:],
                                               op0=ALU.add, op1=ALU.mult).then_inc(rstd_done[i], 1)

            def row_max(t, c):
                dve.wait_ge(approx[c], t.done(2))
                nc.vector.tensor_reduce(x1[(t.at + 1) % 4][:, GH * c:GH * (c + 1), HD],
                                        p_ap[c % 2][:].rearrange("p (h k) -> p h k", h=GH), AX.X, ALU.max,
                                        negate=True).then_inc(maxed[c], 1)

            def step(t):
                q_s = unit[:, 0, :, :].rearrange("p (i k) h -> p i k h", i=2)
                kv_s = p_sum[:, 0, :].rearrange("p (i k h) -> p i k h", i=2, h=HEADS)
                if t.has(-1):
                    dve.wait_ge(out_done, t.done(0))
                    nc.vector.reciprocal(rden[:], pv[:, :, HD]).then_inc(rden_done, 1)
                if t.has(2):
                    dve.wait_ge(cum, t.done(3))
                    dve.wait_ge(yT, t.done(2))
                    nc.vector.tensor_tensor(y[:], q_s, kv_s, ALU.mult).then_inc(straight, 1)
                if t.has(-1):
                    dve.wait_ge(rden_done, t.done(0))
                    nc.vector.tensor_tensor(att[:].rearrange("p (h d) -> p h d", h=HEADS), pv[:, :, 0:HD],
                                            rden[:].unsqueeze(2).to_broadcast([128, HEADS, HD]),
                                            ALU.mult).then_inc(att_done, 1)
                if t.has(2):
                    nc.vector.tensor_tensor(cross[:], q_s[:, :, 1:, :], kv_s[:, ::-1, 1:, :],
                                            ALU.mult).then_inc(crossed, 1)
                if t.has(-1):
                    dve.wait_ge(att_done, t.done(0))
                    nc.vector.tensor_tensor(r2[:].rearrange("p (h d) -> p h d", h=HEADS),
                                            att[:].rearrange("p (h d) -> p h d", h=HEADS),
                                            x1[(t.at - 1) % 4][:, :, 0:HD], ALU.add).then_inc(added[1], 1)
                    dve.wait_ge(added[1], t.done(0))
                    statistics(1, r2)
                if t.has(2):
                    dve.wait_ge(straight, t.done(3))
                    nc.vector.tensor_tensor(y[:, 0, 1:, :], y[:, 0, 1:, :], y[:, 1, 1:, :],
                                            ALU.subtract).then_inc(y_cos, 1)
                if t.has(-1):
                    moments(1, t.done(0))
                if t.has(2):
                    dve.wait_ge(crossed, t.done(3))
                    dve.wait_ge(y_cos, t.done(3))
                    nc.vector.tensor_tensor(y[:, 1, 1:, :], cross[:, 0, :, :], cross[:, 1, :, :],
                                            ALU.add).then_inc(y_done, 1)
                if t.has(3):
                    dve.wait_ge(squared, t.done(4))
                    nc.vector.tensor_reduce(ssq[:].rearrange("p (j h) -> p j h", j=2),
                                            sq[:].rearrange("p (j k h) -> p j h k", j=2, h=HEADS),
                                            AX.X, ALU.add).then_inc(ssq_done, 1)
                if t.has(-1):
                    newton1(1, t.done(0))
                    newton2(1, t.done(0))
                    newton3(1, t.done(0))
                if t.has(1):
                    row_max(t, 0)
                if t.has(-1):
                    dve.wait_ge(rstd_done[1], t.done(0))
                    nc.vector.tensor_scalar(x2[:], r2[:], mv[1][:, 0:1], rstd[1][:], ALU.subtract,
                                            ALU.mult).then_inc(x2_done, 1)
                if t.has(3):
                    dve.wait_ge(rsA_done, t.done(4))
                    nc.vector.scalar_tensor_tensor(out=nA[:], in0=rsA[:], scalar=-0.5, in1=rsA[:], op0=ALU.mult,
                                                   op1=ALU.mult).then_inc(nA1, 1)
                if t.has(-1):
                    dve.wait_ge(x2_done, t.done(0))
                    nc.vector.tensor_scalar(above[:], x2[:], TH_X, None, ALU.is_gt).then_inc(above_done, 1)
                if t.has(3):
                    dve.wait_ge(nA1, t.done(4))
                    nc.vector.tensor_tensor(nA[:], nA[:], ssq[:], ALU.mult).then_inc(nA2, 1)
                if t.has(-1):
                    dve.wait_ge(above_done, t.done(0))
                    nc.vector.scalar_tensor_tensor(out=xq[:], in0=x2[:], scalar=-TH_X, in1=above[:],
                                                   op0=ALU.is_lt, op1=ALU.subtract).then_inc(xq_done, 1)
                if t.has(3):
                    dve.wait_ge(nA2, t.done(4))
                    nc.vector.scalar_tensor_tensor(out=rnA[:], in0=nA[:], scalar=1.5, in1=rsA[:], op0=ALU.add,
                                                   op1=ALU.mult).then_inc(rnA_done, 1)
                if t.has(1):
                    row_max(t, 1)
                if t.has(3):
                    dve.wait_ge(rnA_done, t.done(4))
                    dve.wait_ge(y_done, t.done(3))
                    bank = p_ap[0] if t.b == -2 else p_proj
                    nc.vector.tensor_tensor(unit[:], bank[:].rearrange("p (j k h) -> p j k h", j=2, h=HEADS),
                                            rnA[:].rearrange("p (j h) -> p j h", j=2).unsqueeze(2)
                                            .to_broadcast([128, 2, 2 * BINS, HEADS]), ALU.mult).then_inc(normed, 1)
                if t.has(2):
                    dve.wait_ge(outA, t.done(3))
                    nc.vector.tensor_tensor(r1[:], x_s[(t.at + 2) % 4][:], p_sum[:, 0, :],
                                            ALU.add).then_inc(added[0], 1)
                if t.has(1):
                    row_max(t, 2)
                if t.has(2):
                    dve.wait_ge(added[0], t.done(3))
                    statistics(0, r1)
                if t.has(-1):
                    dve.wait_ge(ffn, t.done(0))
                    nc.vector.tensor_tensor(r3[:], x2[:], p_proj[:, 0:DIM], ALU.add).then_inc(added[2], 1)
                if t.has(2):
                    moments(0, t.done(3))
                if t.has(1):
                    row_max(t, 3)
                if t.has(-1):
                    dve.wait_ge(added[2], t.done(1))
                    statistics(2, r3)
                    moments(2, t.done(0))
                if t.has(2):
                    newton1(0, t.done(3))
                    newton2(0, t.done(3))
                if t.has(-1):
                    newton1(2, t.done(0))
                if t.has(2):
                    newton3(0, t.done(3))
                if t.has(-1):
                    newton2(2, t.done(0))
                if t.has(2):
                    dve.wait_ge(rstd_done[0], t.done(3))
                    nc.vector.tensor_scalar(x1[(t.at + 2) % 4][:, :, 0:HD],
                                            r1[:].rearrange("p (h d) -> p h d", h=HEADS),
                                            mv[0][:, 0:1], rstd[0][:], ALU.subtract, ALU.mult).then_inc(x1_done, 1)
                if t.has(-1):
                    newton3(2, t.done(0))
                    dve.wait_ge(rstd_done[2], t.done(0))
                    nc.vector.scalar_tensor_tensor(out=shift3[:], in0=mv[2][:, 0:1], scalar=-1.0, in1=rstd[2][:],
                                                   op0=ALU.mult, op1=ALU.mult).then_inc(shift_done, 1)

            steps(dve, step)


def dft_tables():
    import numpy as np

    n = np.arange(HD)
    fwd = np.zeros((HEADS, HD, 2, BINS, HEADS))
    inv = np.zeros((HEADS, HD, 2, BINS, HEADS))
    for k in range(BINS):
        for half in range(2):
            if k == 0:
                row, gain = ((-1.0) ** (n * half)) / HD ** 0.5, HD ** 0.5 / HD
            else:
                angle = 2 * np.pi * k * n / HD
                row, gain = (np.sin if half else np.cos)(angle) * (2 / HD) ** 0.5, (HD / 2) ** 0.5 / HD
            for h in range(HEADS):
                fwd[h, :, half, k, h] = row
                inv[h, :, half, k, h] = row * gain
    return (fwd.reshape(DIM, DIM).astype(np.float32), inv.reshape(DIM, DIM).astype(np.float32))


def causal_factors():
    import numpy as np

    q, spare = np.arange(TOK), SLOT - HD
    assert GH * spare * 2 == TOK
    pairs = np.zeros((TOK, GH * spare), np.float32)
    pairs[q, q // 2] = np.where(q % 2, 1.0, FIRST)
    i, k = np.arange(GH * spare)[:, None], np.arange(TOK)[None, :]
    bars = np.where(k > 2 * i + 1, -FAR, np.where(k == 2 * i + 1, -NEAR, 0.0))
    barred = np.zeros((GH, SLOT, TOK), np.float32)
    barred[:, HD:, :] = bars.reshape(GH, spare, TOK)
    return pairs.reshape(TOK, GH, spare), barred.reshape(GH * SLOT, TOK)


def kernel(x, ctx_2048, L0_attn_W_q, L0_attn_W_kv, L0_attn_W_o, L0_ffn_weight, L0_ffn_rram_variation):
    import numpy as np
    import concourse.bacc as bacc
    from concourse.bass_utils import run_bass_kernel_spmd

    x, ctx = np.asarray(x), np.asarray(ctx_2048)
    fwd, inv = dft_tables()
    pairs, barred = causal_factors()
    tok = np.arange(TOK)
    vals = np.zeros((BATCH, TOK, HEADS, SLOT), np.float32)
    vals[..., :HD] = ctx.reshape(BATCH, TOK, HEADS, HD)
    vals[..., HD] = 1.0
    arrays = {
        "x": x,
        "xT": x.reshape(BATCH, TOK, 2, 128).transpose(0, 3, 2, 1),
        "ctxK": ctx.reshape(BATCH, TOK, GROUPS, GH, HD).transpose(0, 3, 4, 2, 1),
        "ctxV": vals,
        "w_q": L0_attn_W_q,
        "w_kv": L0_attn_W_kv,
        "w_oT": np.asarray(L0_attn_W_o).T,
        "ffn_wT": np.asarray(L0_ffn_weight).T,
        "ffn_vT": np.asarray(L0_ffn_rram_variation).T,
        "dft": fwd,
        "idftT": inv,
        "upto": (tok[:, None] <= tok[None, :]).astype(np.float32),
        "pairs": pairs,
        "barred": barred,
        "ident": np.eye(128, dtype=np.float32),
    }
    arrays = {n: np.ascontiguousarray(a) for n, a in arrays.items()}
    nc = bacc.Bacc("TRN2", target_bir_lowering=False, num_devices=1)
    args = [nc.dram_tensor(n, a.shape, mybir.dt.from_np(a.dtype), kind="ExternalInput").ap() for n, a in arrays.items()]
    out = nc.dram_tensor("out", (BATCH, TOK, DIM), mybir.dt.float32, kind="ExternalOutput").ap()
    decoder_layer(nc, *args, out)
    r = run_bass_kernel_spmd(nc, [arrays], core_ids=[0])
    return r.results[0]["out"]
```
